# Optimizing a Trainium2 kernel written in Bass

```python
import numpy as np
import jax
import jax.numpy as jnp

def _softmax(x, axis=-1):
    return jax.nn.softmax(x, axis=axis)

def _gelu(x):
    return jax.nn.gelu(x, approximate=True)

def _silu(x):
    return jax.nn.silu(x)

def _sigmoid(x):
    return jax.nn.sigmoid(x)

def _layernorm(x, axis=-1, eps=1e-05):
    m = jnp.mean(x, axis=axis, keepdims=True)
    v = jnp.var(x, axis=axis, keepdims=True)
    return (x - m) / jnp.sqrt(v + eps)

def _scatter_add(tgt, idx, src, axis=0):
    return tgt.at[idx].add(src)

def _segment_sum(src, seg, n):
    return jax.ops.segment_sum(src, seg, n)
kernel_name = 'mk_flamingo_gated_d1_seqx_r2_f318de'

def setup_inputs(seed: int=0):
    np.random.seed(seed)
    _w = jnp.asarray

    def _rec_inputs():
        import jax
        import jax.numpy as jnp
        _rk = jax.random.key(seed)
        x = -0.000125 + 0.9999 * jax.random.normal(jax.random.fold_in(_rk, 1), (8, 512, 2048), jnp.float32)
        _lenS = 512 - jax.random.randint(jax.random.fold_in(_rk, 7), (8,), 0, max(1, 512 // 4) + 1, jnp.int32)
        _lenS2 = 512 - jax.random.randint(jax.random.fold_in(_rk, 8), (8,), 0, max(1, 512 // 4) + 1, jnp.int32)
        _ctx_4096P = jax.random.normal(jax.random.fold_in(_rk, 11), (8, 16, 2048), jnp.float32)
        _ctx_4096c = jax.random.dirichlet(jax.random.fold_in(_rk, 511), 0.3 * jnp.ones((16,), jnp.float32), (8, 512))
        _ctx_4096t = jnp.einsum('bsk,bkd->bsd', _ctx_4096c, _ctx_4096P)
        _ctx_4096t = _ctx_4096t * jax.lax.rsqrt(jnp.mean(jnp.square(_ctx_4096t)) + 1e-12) * 0.953939
        ctx_4096 = -1.52775e-05 + 0.999936 * (_ctx_4096t + 0.3 * jax.random.normal(jax.random.fold_in(_rk, 611), (8, 512, 2048), jnp.float32))
        _validS = jnp.arange(512)[None, :] < _lenS[:, None]
        _validS2 = jnp.arange(512)[None, :] < _lenS2[:, None]
        _causal = jnp.tril(jnp.ones((512, 512), dtype=bool))
        mask_Bx1x4096_ff1 = jnp.where(jnp.ones((8, 1, 2048), dtype=bool), 1.0, 0.0).astype(jnp.float32)
        _g = jax.random.normal(jax.random.fold_in(_rk, 9001), (2, 1), jnp.float32)
        _g = jnp.sign(_g) * jnp.maximum(jnp.abs(_g), 1.0) + (_g == 0) * 1.0
        g_xattn = _g[0]
        g_ffn = _g[1]
        return (x, ctx_4096, mask_Bx1x4096_ff1, g_xattn, g_ffn)
    x, ctx_4096, mask_Bx1x4096_ff1, g_xattn, g_ffn = _rec_inputs()

    def _L0_xattn_setup():
        import jax, jax.numpy as jnp
        import numpy as np
        W = 128
        H = 8
        D = 512
        DK = D // 2

        def _to_patches(x):
            b, d, s = x.shape
            np_ = s // W
            return x.reshape(b, d, np_, W).transpose(0, 2, 1, 3).reshape(b * np_, d, W)
        key = jax.random.key(seed)
        ks = jax.random.split(key, 10)
        B, S = (8, 2048)
        qk = jax.random.normal(ks[0], (B, D, S), dtype=jnp.float32)
        v = jax.random.normal(ks[1], (B, D, S), dtype=jnp.float32)
        masks = jnp.ones((B, 1, S), dtype=jnp.float32)
        sc = 1.0 / np.sqrt(D)
        Wq = jax.random.normal(ks[2], (DK, D), dtype=jnp.float32) * sc
        bq = jnp.zeros((DK,), dtype=jnp.float32)
        Wk = jax.random.normal(ks[3], (DK, D), dtype=jnp.float32) * sc
        bk = jnp.zeros((DK,), dtype=jnp.float32)
        Wv = jax.random.normal(ks[4], (DK, D), dtype=jnp.float32) * sc
        bv = jnp.zeros((DK,), dtype=jnp.float32)
        Wo = jax.random.normal(ks[5], (D, DK), dtype=jnp.float32) * (1.0 / np.sqrt(DK))
        bo = jnp.zeros((D,), dtype=jnp.float32)
        return dict(qk=qk, v=v, masks=masks, Wq=Wq, bq=bq, Wk=Wk, bk=bk, Wv=Wv, bv=bv, Wo=Wo, bo=bo)
    _L0_xattn_all = _L0_xattn_setup()
    _L0_xattn_in = {k: v for k, v in _L0_xattn_all.items() if k in ('Wq', 'bq', 'Wk', 'bk', 'Wv', 'bv', 'Wo', 'bo')}
    del _L0_xattn_all

    def _L0_ffn_setup():
        import jax, jax.numpy as jnp
        import numpy as np
        K_TOP = 8
        key = jax.random.key(seed)
        k1, k2, k3 = jax.random.split(key, 3)
        B, S, H, E = (4, 2048, 2048, 64)
        hidden_states = jax.random.normal(k1, (B, S, H), dtype=jnp.float32)
        router_weight = jax.random.normal(k2, (E, H), dtype=jnp.float32)
        router_bias = jnp.zeros((E,), dtype=jnp.float32)
        expert_bias = jax.random.normal(k3, (E, H), dtype=jnp.float32) * 0.1
        return {'hidden_states': hidden_states, 'router_weight': router_weight, 'router_bias': router_bias, 'expert_bias': expert_bias}
    _L0_ffn_all = _L0_ffn_setup()
    _L0_ffn_in = {k: v for k, v in _L0_ffn_all.items() if k in ('router_weight', 'router_bias', 'expert_bias')}
    del _L0_ffn_all
    return {'x': x, 'ctx_4096': ctx_4096, 'mask_Bx1x4096_ff1': mask_Bx1x4096_ff1, 'g_xattn': g_xattn, 'g_ffn': g_ffn, 'L0_xattn_Wq': _L0_xattn_in['Wq'], 'L0_xattn_bq': _L0_xattn_in['bq'], 'L0_xattn_Wk': _L0_xattn_in['Wk'], 'L0_xattn_bk': _L0_xattn_in['bk'], 'L0_xattn_Wv': _L0_xattn_in['Wv'], 'L0_xattn_bv': _L0_xattn_in['bv'], 'L0_xattn_Wo': _L0_xattn_in['Wo'], 'L0_xattn_bo': _L0_xattn_in['bo'], 'L0_ffn_router_weight': _L0_ffn_in['router_weight'], 'L0_ffn_router_bias': _L0_ffn_in['router_bias'], 'L0_ffn_expert_bias': _L0_ffn_in['expert_bias']}

def reference(x, ctx_4096, mask_Bx1x4096_ff1, g_xattn, g_ffn, L0_xattn_Wq, L0_xattn_bq, L0_xattn_Wk, L0_xattn_bk, L0_xattn_Wv, L0_xattn_bv, L0_xattn_Wo, L0_xattn_bo, L0_ffn_router_weight, L0_ffn_router_bias, L0_ffn_expert_bias):
    import jax
    import jax.numpy as jnp

    def _L0_xattn_ref(qk, v, masks, Wq, bq, Wk, bk, Wv, bv, Wo, bo):
        import jax, jax.numpy as jnp
        import numpy as np
        W = 128
        H = 8
        D = 512
        DK = D // 2

        def _to_patches(x):
            b, d, s = x.shape
            np_ = s // W
            return x.reshape(b, d, np_, W).transpose(0, 2, 1, 3).reshape(b * np_, d, W)
        B, _, S = qk.shape
        np_ = S // W
        qp = _to_patches(qk)
        vp = _to_patches(v)
        mp = _to_patches(masks)
        q = jnp.einsum('ed,bdw->bew', Wq, qp) + bq[:, None]
        k = jnp.einsum('ed,bdw->bew', Wk, qp) + bk[:, None]
        val = jnp.einsum('ed,bdw->bew', Wv, vp) + bv[:, None]
        BN = q.shape[0]
        dh = DK // H
        qh = q.reshape(BN, H, dh, W)
        kh = k.reshape(BN, H, dh, W)
        vh = val.reshape(BN, H, dh, W)
        scores = jnp.einsum('bhdi,bhdj->bhij', qh, kh) / jnp.sqrt(jnp.asarray(dh, qh.dtype))
        scores = jnp.where(mp[:, :, None, :] > 0, scores, jnp.asarray(-1000000000.0, scores.dtype))
        attn = jax.nn.softmax(scores, axis=-1)
        o = jnp.einsum('bhij,bhdj->bhdi', attn, vh).reshape(BN, DK, W)
        o = jax.nn.gelu(o, approximate=False)
        out = jnp.einsum('de,bew->bdw', Wo, o) + bo[:, None]
        out = out.reshape(B, np_, D, W).transpose(0, 2, 1, 3).reshape(B, D, S)
        out = out * masks
        return out

    def _L0_ffn_ref(hidden_states, router_weight, router_bias, expert_bias):
        import jax, jax.numpy as jnp
        import numpy as np
        K_TOP = 8
        B, S, H = hidden_states.shape
        E = router_weight.shape[0]
        T = B * S
        flat = hidden_states.reshape(T, H)
        logits = jnp.einsum('th,eh->te', flat, router_weight) + router_bias
        scores = jax.nn.softmax(logits, axis=-1)
        topk_w, topk_idx = jax.lax.top_k(scores, K_TOP)
        w_sum = topk_w.sum(axis=-1, keepdims=True)
        w_dense = jnp.zeros((T, E), dtype=scores.dtype).at[jnp.arange(T)[:, None], topk_idx].add(topk_w)
        bias_mix = jnp.einsum('te,eh->th', w_dense, expert_bias)
        out = flat * w_sum + bias_mix
        return out.reshape(B, S, H)
    x = x + jnp.tanh(g_xattn[0]) * _L0_xattn_ref(_layernorm(x, axis=-1), ctx_4096, mask_Bx1x4096_ff1, L0_xattn_Wq, L0_xattn_bq, L0_xattn_Wk, L0_xattn_bk, L0_xattn_Wv, L0_xattn_bv, L0_xattn_Wo, L0_xattn_bo)
    x = x + jnp.tanh(g_ffn[0]) * _L0_ffn_ref(_layernorm(x, axis=-1), L0_ffn_router_weight, L0_ffn_router_bias, L0_ffn_expert_bias)
    return x

_drawn_inputs = setup_inputs


def setup_inputs(seed=0):
    import zlib

    import numpy as np

    out = dict(_drawn_inputs(seed))
    spreads = {'L0_xattn_bq': (0.0, 0.342),
     'L0_xattn_bk': (0.0, 0.8),
     'L0_xattn_bv': (0.0, 0.1),
     'L0_xattn_bo': (0.0, 0.1),
     'L0_ffn_router_bias': (0.0, 0.8)}
    factors = {}
    for name, (base, spread) in spreads.items():
        noise = np.random.default_rng([zlib.crc32(name.encode()), seed]).standard_normal(out[name].shape)
        drawn = base * np.exp(spread * noise) if base else spread * noise
        out[name] = jnp.asarray(drawn.astype(out[name].dtype))
    for name, factor in factors.items():
        out[name] = (out[name] * factor).astype(out[name].dtype)
    return out
```

```python
from contextlib import ExitStack

import concourse.bass as bass
from concourse import mybir

F32 = mybir.dt.float32
F32R = mybir.dt.float32r
BF16 = mybir.dt.bfloat16
F16 = mybir.dt.float16
ALU = mybir.AluOpType
ACT = mybir.ActivationFunctionType
AX = mybir.AxisListType

NB, D, S = 8, 512, 2048
DT = D // 128
E = 256
H, DH = 8, 32
W = 128
U = 256
NU = S // U
SB = S // 128
NX = 64
EPS = 1e-5
SHIFT = 9.0
BIG = 1e9
QSCALE = 1.0 / float(DH) ** 0.5


def bf16_parts(v):
    import numpy as np
    parts, rest = [], np.float32(v)
    for _ in range(3):
        bits = np.array([rest], np.float32).view(np.uint32)
        bits = (bits + 0x7FFF + ((bits >> 16) & 1)) & np.uint32(0xFFFF0000)
        p = bits.view(np.float32)[0]
        parts.append(float(p))
        rest = np.float32(rest - p)
    return parts


class Queues:

    def __init__(self, make):
        self.make, self.sems, self.count = make, {}, {}
        self.list = {e: [] for e in ("sync", "scalar", "vector", "gpsimd", "tensor")}
        self.seen = {e: {} for e in self.list}

    def op(self, eng, sem, fn, *waits, inc=1):
        if sem not in self.sems:
            self.sems[sem], self.count[sem] = self.make(sem), 0
        for name, n in waits:
            if self.seen[eng].get(name, 0) < n:
                self.seen[eng][name] = n
                self.list[eng].append(("wait", name, n))
        self.count[sem] += inc
        self.list[eng].append(("do", fn, sem, inc))
        return sem, self.count[sem]

    def wait(self, eng, *waits):
        for name, n in waits:
            if self.seen[eng].get(name, 0) < n:
                self.seen[eng][name] = n
                self.list[eng].append(("wait", name, n))

    def play(self, eng, e):
        for it in self.list[eng]:
            if it[0] == "wait":
                e.wait_ge(self.sems[it[1]], it[2])
            else:
                it[1](e).then_inc(self.sems[it[2]], it[3])


def gated_block_kernel(nc, x, ctx, mask, g_x, g_f, wqT, wkT, wvT, woT, bq, bk, bv, bo, wrT, rb, eb, out):
    with ExitStack() as st:
        def sb(name, shape, dt=F32):
            return st.enter_context(nc.sbuf_tensor(name, shape, dt))

        def pb(name):
            return st.enter_context(nc.psum_tensor(name, [128, 512], F32))

        Q = Queues(lambda n: st.enter_context(nc.semaphore("s_" + n)))
        op = Q.op

        X = [sb(f"X{i}", [128, DT, S]) for i in range(2)]
        wqk_hi = sb("wqk_hi", [128, DT, 2 * E], F32R)
        wqk_lo = sb("wqk_lo", [128, DT, 2 * E], F32R)
        wv = sb("wv", [128, DT, E])
        wo_hi = sb("wo_hi", [128, 2, D], F32R)
        wo_lo = sb("wo_lo", [128, 2, D], F32R)
        wr2 = sb("wr2", [128, SB, 2 * NX], F32R)
        eb2 = sb("eb2", [128, S], F32R)
        kz_hi = [sb(f"kz_hi{i}", [128, 2, 4, U], F32R) for i in range(2)]
        kz_lo = [sb(f"kz_lo{i}", [128, 2, 4, U], F32R) for i in range(2)]
        z32 = sb("z32", [128, DT, U])
        z_hi = sb("z_hi", [128, DT, U], F32R)
        z_lo = sb("z_lo", [128, DT, U], F32R)
        cx = [sb(f"cx{i}", [128, DT, W]) for i in range(3)]
        q_hi = [sb(f"q_hi{i}", [128, 2, U], F32R) for i in range(2)]
        q_lo = [sb(f"q_lo{i}", [128, 2, U], F32R) for i in range(2)]
        k32 = sb("k32", [128, 2, U])
        k_hi = sb("k_hi", [128, 2, U], F32R)
        k_lo = sb("k_lo", [128, 2, U], F32R)
        NP = 2
        P32 = [sb(f"P32_{i}", [128, 4, W]) for i in range(NP)]
        pt_hi = [sb(f"pt_hi{i}", [128, 4, W], F16) for i in range(2)]
        pt_lo = [sb(f"pt_lo{i}", [128, 4, W], F16) for i in range(2)]
        NV = 3
        v32 = sb("v32", [128, H, DH])
        vp = [[sb(f"v{k}_{i}", [128, H, DH + 1], BF16) for k in range(3)] for i in range(NV)]
        o32 = [sb(f"o32_{i}", [128, 2, E]) for i in range(2)]
        ot_hi = sb("ot_hi", [128, 2, U], F32R)
        ot_lo = sb("ot_lo", [128, 2, U], F32R)
        hc = [sb(f"hc{i}", [128, 2, U]) for i in range(2)]
        ht_hi = sb("ht_hi", [128, 2, U], F32R)
        ht_lo = sb("ht_lo", [128, 2, U], F32R)
        rows = [sb(f"rows{i}", [128, S], BF16) for i in range(2)]
        mk = [sb(f"mk{i}", [128, U]) for i in range(2)]
        ident = sb("ident", [128, 128])
        id2 = sb("id2", [128, NX])
        ones3 = sb("ones3", [128, 128], BF16)
        bo6 = sb("bo6", [128, D], BF16)
        cst = sb("cst", [128, 24])
        bvb = sb("bvb", [128, E])
        rbb = sb("rbb", [128, NX])
        tgm = sb("tgm", [128, 128])
        bnst = sb("bnst", [128, DT, 4, 6])
        mv = sb("mv", [128, DT, 2])
        bn2 = sb("bn2", [128, DT, 4, 6])
        mv2 = sb("mv2", [128, DT, 2])
        ln1 = [sb(f"ln1_{i}", [128, 3, DT]) for i in range(2)]
        ln2 = sb("ln2", [128, 3, DT])
        mx = sb("mx", [128, 4, 4])
        rc = sb("rc", [128, 2, H])
        L = sb("L", [128, U])
        lg = sb("lg", [128, 2, NX])
        lr = sb("lr", [128, 2, NX])
        ex = sb("ex", [128, 2, NX])
        w2 = sb("w2", [128, 2, 2 * NX])
        t8 = sb("t8", [128, 2, 8])
        sc = sb("sc", [128, 2, 8])
        wt_hi = sb("wt_hi", [128, 2, 128], F32R)
        wt_lo = sb("wt_lo", [128, 2, 128], F32R)
        half = sb("half", [128, DT])

        NR = 6
        ring = [pb(f"ring{i}") for i in range(NR)]
        freed = [() for _ in range(NR)]
        turn = [0]
        PO = pb("PO")
        PR = pb("PR")

        def take():
            i = turn[0] % NR
            turn[0] += 1
            assert freed[i] is not None, "a bank is taken before its readers are queued"
            w, freed[i] = freed[i], None
            return i, ring[i], w

        def mm(*parts):
            def fn(e):
                for o, a, b, s0, s1 in parts:
                    last = e.matmul(o, a, b, start=s0, stop=s1)
                return last
            return fn

        def tr(*parts):
            def fn(e):
                for o, a, i in parts:
                    last = e.transpose(o, a, i)
                return last
            return fn

        def f32(ap):
            return ap.bitcast(F32)

        BQ, BK, TG, TF, SH, M05 = 0, 2, 4, 5, 6, 7

        stage = X[1]
        wst = stage[:, 0, :].rearrange("p (k n) -> p k n", k=DT)

        def load(sem, dst, src, *waits):
            return op("sync", sem, lambda e: e.dma_start(dst, src), *waits, inc=16)

        xv = x.rearrange("b (t p) s -> b t p s", p=128)
        ov = out.rearrange("b (t p) s -> b t p s", p=128)
        cv = ctx.rearrange("b (t p) s -> b p t s", p=128)
        mflat = mask.rearrange("b o s -> (b o) s")

        load("w_x", cst[:, TG:TG + 1], g_x[None, :].to_broadcast([128, 1]))
        load("w_x", cst[:, TF:TF + 1], g_f[None, :].to_broadcast([128, 1]))
        load("w_x", cst[:, BQ:BQ + 2], bq)
        t_small = load("w_x", cst[:, BK:BK + 2], bk)
        x_in = [[load(f"x{i}_{t}", X[0][:, t, :], xv[0, t]) for t in range(DT)] if i == 0 else None for i in range(2)]
        load("w_qk", wst[:, :, 0:E], wqT.rearrange("(k p) n -> p k n", p=128))
        t_qk = load("w_qk", wst[:, :, E:2 * E], wkT.rearrange("(k p) n -> p k n", p=128))
        t_wv = load("w_v", wv[:], wvT.rearrange("(k p) n -> p k n", p=128))
        t_bv = load("w_v", bvb[:], bv[None, :].to_broadcast([128, E]))
        mT = stage[:, 1, 0:128]
        t_mT = load("w_mT", mT, mflat.rearrange("b (w i) -> (b w) i", i=128))
        mneg = stage[:, 1, 640:768]
        wost = stage[:, 1, 1024:2048].rearrange("p (k n) -> p k n", k=2)
        t_wo = load("w_o", wost, woT.rearrange("(k p) n -> p k n", p=128))
        bost = stage[0:6, 2, 0:512]
        t_bo = load("w_bo", bost, bo[None, :].to_broadcast([6, D]))
        t_rb = load("w_rb", rbb[:], rb[None, :].to_broadcast([128, NX]))
        wrst = stage[:, 3, 0:1024].rearrange("p (k n) -> p k n", k=SB)
        t_wr = load("w_r", wrst, wrT.rearrange("(k p) n -> p k n", p=128))

        def G(sem, fn, *w):
            return op("gpsimd", sem, fn, *w)

        def V(sem, fn, *w):
            return op("vector", sem, fn, *w)

        def A(sem, fn, *w):
            return op("scalar", sem, fn, *w)

        def T(sem, fn, *w):
            return op("tensor", sem, fn, *w)

        a = G("g_set", lambda e: e.memset(ident[:], 0.0))
        t_id = G("g_set", lambda e: e.affine_select(out=ident[:], in_=ident[:], compare_op=ALU.not_equal, fill=1.0,
                                                   base=0, pattern=[[-1, 128]], channel_multiplier=1), a)
        b = G("g_set", lambda e: e.memset(id2[:], 0.0))
        b = G("g_set", lambda e: e.affine_select(out=id2[:], in_=id2[:], compare_op=ALU.not_equal, fill=1.0,
                                                 base=0, pattern=[[-1, NX]], channel_multiplier=1), b)
        t_id2 = G("g_set", lambda e: e.affine_select(out=id2[:], in_=id2[:], compare_op=ALU.not_equal, fill=1.0,
                                                     base=-NX, pattern=[[-1, NX]], channel_multiplier=1), b)
        G("g_set", lambda e: e.memset(half[:], -0.5))
        t_cst = G("g_set", lambda e: e.memset(cst[:, SH:SH + 1], SHIFT))
        t_vone = [G("g_set", lambda e, i=i, k=k: e.memset(vp[i][k][:, :, DH:DH + 1], 1.0 if k == 0 else 0.0))
                  for i in range(NV) for k in range(3)][-1]
        a = V("v_set", lambda e: e.memset(ones3[:], 1.0))
        bz = V("v_set", lambda e: e.memset(bo6[:], 0.0))
        for i in range(2):
            t_rz = V("v_set", lambda e, i=i: e.memset(rows[i][:], 0.0))
        for i in range(2):
            V("v_set", lambda e, i=i: e.memset(f32(kz_hi[i][:]), 0.0))
            t_kz0 = V("v_set", lambda e, i=i: e.memset(f32(kz_lo[i][:]), 0.0))
        a = G("g_set", lambda e: e.affine_select(out=ones3[:], in_=ones3[:], compare_op=ALU.is_ge, fill=0.0,
                                                 base=-6, pattern=[[0, 128]], channel_multiplier=1), a)
        t_ones3 = G("g_set", lambda e: e.affine_select(out=ones3[:], in_=ones3[:], compare_op=ALU.is_ge, fill=0.0,
                                                       base=8, pattern=[[0, 128]], channel_multiplier=-1), a)

        t_tg = A("a_set", lambda e: e.activation(cst[:, TG:TG + 2], cst[:, TG:TG + 2], ACT.Tanh), t_small)
        t_bq = V("v_set", lambda e: e.tensor_scalar(cst[:, BQ:BQ + 2], cst[:, BQ:BQ + 2], QSCALE, None, ALU.mult), t_small)

        def stats1(b, t, r, xin):
            return V("bn1", lambda e: e.bn_stats(bnst[:, t, r, :], X[b % 2][:, t, r * 512:(r + 1) * 512]), xin)

        def norm1(b, last, free):
            l = ln1[b % 2]
            for t in range(DT):
                v = V("bn1a", lambda e, t=t: e.bn_aggr(mv[:, t, :], bnst[:, t, :, :].rearrange("p a c -> p (a c)")), last, free)
            V("bn1b", lambda e: e.tensor_scalar(l[:, 0, :], mv[:, :, 0], -1.0, None, ALU.mult), v)
            v = V("bn1b", lambda e: e.tensor_scalar(l[:, 1, :], mv[:, :, 1], EPS, None, ALU.add))
            return G("rstd1", lambda e: e.tensor_tensor(l[:, 2, :], l[:, 1, :], half[:], ALU.pow), v)

        for t in range(DT):
            for r in range(4):
                last = stats1(0, t, r, x_in[0][t])
        n1 = {0: norm1(0, last, t_cst)}

        V("v_w", lambda e: e.tensor_scalar(wst[:, :, 0:E], wst[:, :, 0:E], QSCALE, None, ALU.mult), t_qk)
        a = V("v_w", lambda e: e.tensor_copy(wqk_hi[:, :, E:2 * E], wst[:, :, E:2 * E]))
        a = V("v_w", lambda e: e.tensor_copy(wqk_hi[:, :, 0:E], wst[:, :, 0:E]), a)
        t_wqk = V("v_w", lambda e: e.tensor_tensor(wqk_lo[:], wst, f32(wqk_hi[:]), ALU.subtract), a)
        a = A("a_w", lambda e: e.activation(wo_hi[:], wost, ACT.Copy), t_wo)
        t_wos = V("v_w", lambda e: e.tensor_tensor(wo_lo[:], wost, f32(wo_hi[:]), ALU.subtract), a)
        a = A("a_w", lambda e: e.activation(wr2[:, :, 0:NX], wrst, ACT.Copy), t_wr)
        t_wrs = V("v_w", lambda e: e.tensor_tensor(wr2[:, :, NX:2 * NX], wrst, f32(wr2[:, :, 0:NX]), ALU.subtract), a)
        bp = [stage[0:6, 3, 1024 + 256 * k:1280 + 256 * k].bitcast(BF16) for k in range(3)]
        a = V("v_w", lambda e: e.tensor_copy(bp[0], bost), t_bo)
        a = V("v_w", lambda e: e.tensor_tensor(bost, bost, bp[0], ALU.subtract), a)
        a = V("v_w", lambda e: e.tensor_copy(bp[1], bost), a)
        a = V("v_w", lambda e: e.tensor_tensor(bp[2], bost, bp[1], ALU.subtract), a)
        for r, k in enumerate((0, 0, 1, 1, 0, 2)):
            t_bo6 = load("bo6", bo6[r:r + 1, :], bp[k][r:r + 1, :], a, bz)
        tgr = stage[:, 1, 128:256]
        keep = stage[:, 1, 256:640].bitcast(BF16).rearrange("p (k i) -> p k i", k=6)
        rows_d = nc.dram_tensor("rows_d", (6, 128, 128), BF16, kind="Internal").ap()
        V("v_m", lambda e: e.tensor_scalar(tgr, mT, cst[:, TG:TG + 1], None, ALU.mult), t_mT, t_tg)
        a = V("v_m", lambda e: e.tensor_scalar(mneg, mT, 0.0, 1.0, ALU.is_gt, ALU.subtract))
        for k, part in enumerate(bf16_parts(BIG)):
            V("v_m", lambda e, k=k, part=part: e.tensor_scalar(keep[:, 3 + k, :], mneg, part, None, ALU.mult), a)
        a = V("v_m", lambda e: e.tensor_copy(keep[:, 0, :], tgr), a)
        a = V("v_m", lambda e: e.tensor_tensor(tgr, tgr, keep[:, 0, :], ALU.subtract), a)
        a = V("v_m", lambda e: e.tensor_copy(keep[:, 1, :], tgr), a)
        a = V("v_m", lambda e: e.tensor_tensor(keep[:, 2, :], tgr, keep[:, 1, :], ALU.subtract), a)
        t_keep = load("rows_d", rows_d.rearrange("k p i -> p k i"), keep, a)
        i, bank, w = take()
        a = T("setT", lambda e, bank=bank: e.transpose(bank[:, 0:128], mT, ident[:]), t_mT, t_id, *w)
        t_tgm = V("v_m", lambda e, bank=bank: e.tensor_scalar(tgm[:], bank[:, 0:128], cst[:, TG:TG + 1], None, ALU.mult), a, t_tg)
        freed[i] = (t_tgm,)
        ebst = stage[:, 2, :]
        load("w_eb", ebst[0:NX, :], eb, t_bo6)
        t_eb = load("w_eb", ebst[NX:128, :], eb)
        a = A("a_w", lambda e: e.activation(eb2[:], ebst, ACT.Copy), t_eb)
        t_ebs = V("v_w", lambda e: e.tensor_tensor(eb2[NX:128, :], ebst[NX:128, :], f32(eb2[NX:128, :]), ALU.subtract), a)
        staged = (t_ebs, t_tgm, t_keep, t_wos, t_wrs, t_wqk)

        def load_rows(b, *free):
            t = None
            for r, k in enumerate((0, 1, 0, 1, 2, 0, 3, 4, 5)):
                t = load(f"rows{b % 2}", rows[b % 2][r:r + 1, :], rows_d[k:k + 1, b * 16:(b + 1) * 16, :].rearrange("o w i -> o (w i)"), t_keep, t_rz, *free)
            return t

        rows_in = {0: load_rows(0)}
        x1_done, bn2_last = {}, None
        for t in range(DT):
            x_in[1] = x_in[1] or []
            x_in[1].append(load(f"x1_{t}", X[1][:, t, :], xv[1, t], *staged))
        xin = {0: x_in[0], 1: x_in[1]}

        st_ = {}

        def load_ctx(p):
            b, w = divmod(p, S // W)
            i = p % 3
            free = (st_["v", p - 3],) if p >= 3 else ()
            st_["cx", p] = load(f"cx{i}", cx[i][:], cv[b][:, :, w * W:(w + 1) * W], *free)

        def load_mask(u):
            b, c = divmod(u, NU)
            i = u % 2
            free = (st_["k32", u - 2],) if u >= 2 else ()
            t = load(f"mk{i}", mk[i][:], mflat[b:b + 1, c * U:(c + 1) * U].to_broadcast([128, U]), *free)
            st_["mk", u] = G("mk01", lambda e: e.tensor_scalar(mk[i][:], mk[i][:], 0.0, None, ALU.is_gt), t)

        def normalise(u):
            b, c = divmod(u, NU)
            l = ln1[b % 2]
            free = (st_["z_lo", u - 1],) if u else ()
            for t in range(DT):
                z = G("z32", lambda e, t=t: e.tensor_scalar(z32[:, t, :], X[b % 2][:, t, c * U:(c + 1) * U],
                                                            l[:, 0, t:t + 1], l[:, 2, t:t + 1], ALU.add, ALU.mult),
                      n1[b], *free)
            free = (st_["qk", u - 1],) if u else ()
            h = A("z_hi", lambda e: e.activation(z_hi[:], z32[:], ACT.Copy), z, *free)
            st_["z_hi", u] = h
            st_["z_lo", u] = V("z_lo", lambda e: e.tensor_tensor(z_lo[:], z32[:], f32(z_hi[:]), ALU.subtract), h, z, *free)

        def project(u, col):
            i, bank, w = take()
            parts = []
            for m in range(2):
                o = bank[:, m * U:(m + 1) * U]
                n = 0
                for t in range(DT):
                    cols = slice(col + m * 128, col + (m + 1) * 128)
                    for a_, z_ in ((wqk_hi, z_hi), (wqk_lo, z_hi), (wqk_hi, z_lo)):
                        parts.append((o, a_[:, t, cols], z_[:, t, :], n == 0, n == 3 * DT - 1))
                        n += 1
            t = T("qk", mm(*parts), st_["z_hi", u], st_["z_lo", u], t_wqk, *w)
            st_["qk", u] = t
            return i, bank, t

        def queries(u):
            i, bank, t = project(u, 0)
            qh, ql = q_hi[u % 2], q_lo[u % 2]
            free = (st_["S", 4 * (u - 2) + 3],) if u >= 2 else ()
            for m in range(2):
                o = bank[:, m * U:(m + 1) * U]
                h = A("q_hi", lambda e, m=m, o=o: e.activation(qh[:, m, :], o, ACT.Identity, bias=cst[:, BQ + m:BQ + m + 1]),
                      t, t_bq, *free)
            for m in range(2):
                o = bank[:, m * U:(m + 1) * U]
                l = V("q_lo", lambda e, m=m, o=o: e.scalar_tensor_tensor(
                    out=ql[:, m, :], in0=o, scalar=cst[:, BQ + m:BQ + m + 1], in1=f32(qh[:, m, :]),
                    op0=ALU.add, op1=ALU.subtract), h, t_bq, *free)
            freed[i] = (h, l)
            st_["q", u] = (h, l)

        def keys(u):
            i, bank, t = project(u, E)
            free = (st_["k_lo", u - 1],) if u else ()
            for m in range(2):
                o = bank[:, m * U:(m + 1) * U]
                v = V("k32", lambda e, m=m, o=o: e.scalar_tensor_tensor(
                    out=k32[:, m, :], in0=o, scalar=cst[:, BK + m:BK + m + 1], in1=mk[u % 2][:],
                    op0=ALU.add, op1=ALU.mult), t, st_["mk", u], *free)
            freed[i] = (v,)
            st_["k32", u] = v
            free = st_.get(("kz", u - 1), ())
            h = A("k_hi", lambda e: e.activation(k_hi[:], k32[:], ACT.Copy), v, *free)
            l = V("k_lo", lambda e: e.tensor_tensor(k_lo[:], k32[:], f32(k_hi[:]), ALU.subtract), h, v, *free)
            st_["k_lo", u] = l
            free = (st_["S", 4 * (u - 2) + 3],) if u >= 2 else (t_kz0,)
            toks = []
            for n, (src, dst, tok) in enumerate(((k_hi, kz_hi[u % 2], h), (k_lo, kz_lo[u % 2], l))):
                for g in range(4):
                    q = load(f"kz{u % 2}_{n}", f32(dst[32 * g:32 * g + 32, :, g, :]), f32(src[32 * g:32 * g + 32, :, :]), tok, *free)
                toks.append(q)
            st_["kz", u] = tuple(toks)

        def values(p):
            i, bank, w = take()
            c = cx[p % 3]
            t = T("v", mm(*[(bank[:, 0:E], c[:, k, :], wv[:, k, :], k == 0, k == DT - 1) for k in range(DT)]),
                  st_["cx", p], t_wv, *w)
            st_["v", p] = t
            vv = vp[p % NV]
            free = (st_["PV", 2 * (p - NV) + 1],) if p >= NV else (t_vone,)
            ps = bank[:, 0:E].rearrange("p (h d) -> p h d", h=H)
            bb = bvb[:].rearrange("p (h d) -> p h d", h=H)
            prev = (st_["v3", p - 1],) if p else ()
            a = V("v32", lambda e: e.tensor_tensor(v32[:], ps, bb, ALU.add), t, t_bv, *prev)
            freed[i] = (a,)
            b = A("v1", lambda e: e.activation(vv[0][:, :, 0:DH], v32[:], ACT.Copy), a, *free)
            c_ = V("vr", lambda e: e.tensor_tensor(v32[:], v32[:], vv[0][:, :, 0:DH], ALU.subtract), b, a)
            d = A("v2", lambda e: e.activation(vv[1][:, :, 0:DH], v32[:], ACT.Copy), c_)
            st_["v3", p] = V("v3", lambda e: e.tensor_tensor(vv[2][:, :, 0:DH], v32[:], vv[1][:, :, 0:DH], ALU.subtract), d, c_, *free)
            st_["v2", p] = d

        def scores(s):
            u, k = divmod(s, 4)
            w, m = divmod(k, 2)
            i, bank, fr = take()
            c = (u % NU) * U + w * W
            kh = kz_hi[u % 2][:, m, :, w * W:(w + 1) * W]
            kl = kz_lo[u % 2][:, m, :, w * W:(w + 1) * W]
            qh = q_hi[u % 2][:, m, w * W:(w + 1) * W]
            ql = q_lo[u % 2][:, m, w * W:(w + 1) * W]
            b = u // NU
            mrow = rows[b % 2][:, c:c + W].unsqueeze(1).to_broadcast([128, 4, W])
            o = bank[:].rearrange("p (h j) -> p h j", h=4)
            t = T("S", mm((o, ones3[:], mrow, True, False), (o, qh, kh, False, False), (o, ql, kh, False, False),
                          (o, qh, kl, False, True)), *st_["q", u], *st_["kz", u], rows_in[b], t_ones3, *fr)
            st_["S", s] = t
            P = P32[s % NP]
            mm_ = mx[:, s % 4, :]
            v = V("mx", lambda e: e.tensor_reduce(mm_, o, AX.X, ALU.max), t)
            free = (st_["PT", s - NP],) if s >= NP else ()
            v = V("sub", lambda e: e.tensor_tensor(P[:], o, mm_.unsqueeze(2).to_broadcast([128, 4, W]), ALU.subtract),
                  v, *free)
            freed[i] = (v,)
            st_["exp", s] = A("exp", lambda e: e.activation(P[:], P[:], ACT.Exp, bias=cst[:, SH:SH + 1]), v, t_cst)

        def turn_p(s):
            i, bank, fr = take()
            P = P32[s % NP]
            t = T("PT", tr(*[(bank[:, h * W:(h + 1) * W], P[:, h, :], ident[:]) for h in range(4)]),
                  st_["exp", s], t_id, *fr)
            st_["PT", s] = t
            o = bank[:].rearrange("p (h j) -> p h j", h=4)
            free = (st_["PV", s - 2],) if s >= 2 else ()
            h = A("pt_hi", lambda e: e.activation(pt_hi[s % 2][:], o, ACT.Copy), t, *free)
            l = V("pt_lo", lambda e: e.tensor_tensor(pt_lo[s % 2][:], o, pt_hi[s % 2][:], ALU.subtract), h, t, *free)
            freed[i] = (h, l)
            st_["pt", s] = (h, l)

        def weigh(s):
            u, k = divmod(s, 4)
            w, m = divmod(k, 2)
            p = 2 * u + w
            vv = vp[p % NV]
            ph, pl = pt_hi[s % 2], pt_lo[s % 2]
            parts = []
            for h in range(4):
                hh = 4 * m + h
                o = PO[:, hh * (DH + 1):(hh + 1) * (DH + 1)]
                for n, (a, k_) in enumerate(((ph, 0), (ph, 1), (ph, 2), (pl, 0), (pl, 1))):
                    parts.append((o, a[:, h, :], vv[k_][:, hh, :], n == 0, n == 4))
            free = (st_["on", p - 1],) if m == 0 and p else ()
            t = T("PV", mm(*parts), *st_["pt", s], st_["v3", p], st_["v2", p], *free)
            st_["PV", s] = t
            if m:
                o = PO[:, 0:H * (DH + 1)].rearrange("p (h d) -> p h d", h=H)
                r = rc[:, p % 2, :].unsqueeze(2)
                v = V("rc", lambda e: e.reciprocal(r, o[:, :, DH:DH + 1]), t)
                od = o32[u % 2][:, w, :].rearrange("p (h d) -> p h d", h=H)
                free = (st_["OT", u - 2],) if u >= 2 else ()
                st_["on", p] = V("on", lambda e: e.tensor_tensor(od, o[:, :, 0:DH], r.to_broadcast([128, H, DH]), ALU.mult),
                                 v, *free)

        def gelu(u):
            o = o32[u % 2]
            a = A("gelu", lambda e: e.activation(o[:], o[:], ACT.Gelu), st_["on", 2 * u + 1])
            for w in range(2):
                p = 2 * u + w
                st_["g2", u] = G("g2", lambda e, w=w, p=p: e.tensor_scalar(o[:, w, :], o[:, w, :], tgm[:, p:p + 1], None,
                                                                          ALU.mult), a, t_tgm)

        def turn_o(u):
            i, bank, fr = take()
            t = T("OT", tr(*[(bank[:, m * U + w * W:m * U + (w + 1) * W], o32[u % 2][:, w, m * 128:(m + 1) * 128], ident[:])
                             for m in range(2) for w in range(2)]), st_["g2", u], t_id, *fr)
            st_["OT", u] = t
            free = (st_["WO", u - 1],) if u else ()
            o = bank[:].rearrange("p (m i) -> p m i", m=2)
            h = A("ot_hi", lambda e: e.activation(ot_hi[:], o, ACT.Copy), t, *free)
            l = V("ot_lo", lambda e: e.tensor_tensor(ot_lo[:], o, f32(ot_hi[:]), ALU.subtract), h, t, *free)
            freed[i] = (h, l)
            st_["ot", u] = (h, l)

        def project_out(u, j):
            b, c = divmod(u, NU)
            i, bank, fr = take()
            parts = []
            for n in range(2):
                t = 2 * j + n
                o = bank[:, n * U:(n + 1) * U]
                cols = slice(t * 128, (t + 1) * 128)
                parts.append((o, bo6[:, cols], rows[b % 2][:, c * U:(c + 1) * U], True, False))
                for m in range(2):
                    for q_, (a, z) in enumerate(((wo_hi, ot_hi), (wo_lo, ot_hi), (wo_hi, ot_lo))):
                        parts.append((o, a[:, m, cols], z[:, m, :], False, m == 1 and q_ == 2))
            t = T("WO", mm(*parts), *st_["ot", u], rows_in[b], t_bo6, t_wos, *fr)
            st_["WO", u] = t
            xs = X[b % 2][:, 2 * j:2 * j + 2, c * U:(c + 1) * U]
            v = V("x1", lambda e: e.tensor_tensor(xs, xs, bank[:].rearrange("p (n i) -> p n i", n=2), ALU.add), t)
            freed[i] = (v,)
            st_["x1", u, j] = v

        def stats2(b, r):
            for t in range(DT):
                st_["bn2", b] = V("bn2", lambda e, t=t: e.bn_stats(bn2[:, t, r, :], X[b % 2][:, t, r * 512:(r + 1) * 512]),
                                  st_["x1", b * NU + 2 * r + 1, 1], *((st_["mv2", b - 1],) if b else ()))

        def norm2(b):
            for t in range(DT):
                v = V("mv2", lambda e, t=t: e.bn_aggr(mv2[:, t, :], bn2[:, t, :, :].rearrange("p a c -> p (a c)")),
                      st_["bn2", b])
            st_["mv2", b] = v
            free = (st_["ac", b - 1, 1],) if b else ()
            V("ln2", lambda e: e.tensor_scalar(ln2[:, 0, :], mv2[:, :, 0], -1.0, None, ALU.mult), v, *free)
            v = V("ln2", lambda e: e.tensor_scalar(ln2[:, 1, :], mv2[:, :, 1], EPS, None, ALU.add))
            st_["ln2", b] = G("rstd2", lambda e: e.tensor_tensor(ln2[:, 2, :], ln2[:, 1, :], half[:], ALU.pow), v)

        def route(b, j, c):
            n = (b * 2 + j) * NU + c
            hh = hc[n % 2]
            free = (st_["hT", n - 2],) if n >= 2 else ()
            for q_ in range(2):
                t = 2 * j + q_
                g = G("h", lambda e, q_=q_, t=t: e.tensor_scalar(
                    hh[:, q_, :], X[b % 2][:, t, c * U:(c + 1) * U], ln2[:, 0, t:t + 1], ln2[:, 2, t:t + 1],
                    ALU.add, ALU.mult), st_["ln2", b], *free)
            st_["h", n] = g

        def route_t(b, j, c):
            n = (b * 2 + j) * NU + c
            hh = hc[n % 2]
            i, bank, fr = take()
            t = T("hT", tr(*[(bank[:, a * U + q_ * 128:a * U + (q_ + 1) * 128], hh[:, q_, a * 128:(a + 1) * 128], ident[:])
                             for a in range(2) for q_ in range(2)]), st_["h", n], t_id, *fr)
            st_["hT", n] = t
            o = bank[:].rearrange("p (a i) -> p a i", a=2)
            free = (st_["R", n - 1],) if n else ()
            h = A("ht_hi", lambda e: e.activation(ht_hi[:], o, ACT.Copy), t, *free)
            l = V("ht_lo", lambda e: e.tensor_tensor(ht_lo[:], o, f32(ht_hi[:]), ALU.subtract), h, t, *free)
            freed[i] = (h, l)
            st_["ht", n] = (h, l)

        def route_r(b, j, c):
            n = (b * 2 + j) * NU + c
            parts = []
            for a in range(2):
                for q_, z in enumerate((ht_hi, ht_lo)):
                    parts.append((PR[:, 0:U], wr2[:, 2 * c + a, :], z[:, a, :], c == 0 and a == 0 and q_ == 0,
                                  c == NU - 1 and a == 1 and q_ == 1))
            free = (st_["L", b * 2 + j - 1],) if c == 0 and n else ()
            st_["R", n] = T("R", mm(*parts), *st_["ht", n], t_wrs, *free)

        def choose(b, j):
            n = b * 2 + j
            free = (st_["LT", n - 1],) if n else ()
            st_["L", n] = A("L", lambda e: e.activation(L[:], PR[:, 0:U], ACT.Copy), st_["R", n * NU + NU - 1], *free)
            i, bank, fr = take()
            t = T("LT", mm(*[(bank[:, q_ * NX:(q_ + 1) * NX], L[:, q_ * 128:(q_ + 1) * 128], id2[:], True, True)
                             for q_ in range(2)]), st_["L", n], t_id2, *fr)
            st_["LT", n] = t
            free = (st_["wT", n - 1],) if n else ()
            v = V("lg", lambda e: e.tensor_tensor(lg[:], bank[:, 0:2 * NX].rearrange("p (q x) -> p q x", q=2),
                                                  rbb[:].unsqueeze(1).to_broadcast([128, 2, NX]), ALU.add), t, t_rb)
            freed[i] = (v,)
            for q_ in range(2):
                r = 2 * j + q_
                m8_ = t8[:, q_, :]
                s_ = sc[:, q_, :]
                v1 = V("top", lambda e, q_=q_, m8_=m8_: e.max(m8_, lg[:, q_, :]), v)
                v2 = V("top", lambda e, m8_=m8_, s_=s_: e.tensor_scalar(s_[:, 0:1], m8_[:, 0:1], -1.0, None, ALU.mult), v1)
                ea = A("ex", lambda e, q_=q_, s_=s_: e.activation(ex[:, q_, :], lg[:, q_, :], ACT.Exp, bias=s_[:, 0:1],
                                                                 accum_out=s_[:, 1:2]), v2)
                v3 = V("top", lambda e, q_=q_, m8_=m8_: e.match_replace(lr[:, q_, :], m8_, lg[:, q_, :], -3.0e38), v1)
                v3 = V("top", lambda e, q_=q_: e.tensor_tensor(lr[:, q_, :], lr[:, q_, :], lg[:, q_, :], ALU.not_equal), v3)
                v3 = V("top", lambda e, q_=q_: e.tensor_tensor(ex[:, q_, :], ex[:, q_, :], lr[:, q_, :], ALU.mult), v3, ea)
                v3 = V("top", lambda e, q_=q_, s_=s_: e.tensor_reduce(s_[:, 2:3], ex[:, q_, :], AX.X, ALU.add), v3)
                v4 = V("top", lambda e, s_=s_: e.reciprocal(s_[:, 3:4], s_[:, 1:2]), ea)
                v4 = V("top", lambda e, s_=s_: e.tensor_scalar(s_[:, 4:5], s_[:, 3:4], cst[:, TF:TF + 1], None, ALU.mult), v4, t_tg)
                v5 = V("top", lambda e, q_=q_, s_=s_: e.tensor_scalar(
                    w2[:, q_, :].rearrange("p (a x) -> p a x", a=2), ex[:, q_, :].unsqueeze(1).to_broadcast([128, 2, NX]),
                    s_[:, 4:5], None, ALU.mult), v3, v4, *free)
                v6 = V("top", lambda e, s_=s_: e.tensor_scalar(s_[:, 5:6], s_[:, 2:3], s_[:, 4:5], None, ALU.mult), v3, v4)
                v6 = V("top", lambda e, s_=s_, r=r: e.tensor_scalar(s_[:, 5:6], s_[:, 5:6], ln2[:, 2, r:r + 1], None, ALU.mult),
                       v6, st_["ln2", b])
                v7 = V("top", lambda e, s_=s_: e.tensor_scalar(s_[:, 6:7], s_[:, 5:6], 1.0, None, ALU.add), v6)
                v7 = V("top", lambda e, s_=s_, r=r: e.tensor_scalar(s_[:, 7:8], s_[:, 5:6], ln2[:, 0, r:r + 1], None, ALU.mult), v6)
            st_["ac", b, j] = v7
            st_["w2", n] = v5

        def spread(b, j):
            n = b * 2 + j
            i, bank, fr = take()
            t = T("wT", tr(*[(bank[:, q_ * 128:(q_ + 1) * 128], w2[:, q_, :], ident[:]) for q_ in range(2)]),
                  st_["w2", n], t_id, *fr)
            st_["wT", n] = t
            o = bank[:, 0:256].rearrange("p (q t) -> p q t", q=2)
            free = (st_["mix", n - 1],) if n else ()
            h = A("wt_hi", lambda e: e.activation(wt_hi[:], o, ACT.Copy), t, *free)
            l = V("wt_lo", lambda e: e.tensor_tensor(wt_lo[:], o, f32(wt_hi[:]), ALU.subtract), h, t, *free)
            freed[i] = (h, l)
            st_["wt", n] = (h, l)
            for q_ in range(2):
                xs = X[b % 2][:, 2 * j + q_, :]
                st_["xa", b, 2 * j + q_] = G("xa", lambda e, q_=q_, xs=xs: e.tensor_scalar(
                    xs, xs, sc[:, q_, 6:7], sc[:, q_, 7:8], ALU.mult, ALU.add),
                    st_["ac", b, j], st_["hT", n * NU + NU - 1])

        def mix(b, j, q_, c):
            n = b * 2 + j
            t_ = 2 * j + q_
            i, bank, fr = take()
            cols = slice(c * 512, (c + 1) * 512)
            t = T("mix", mm((bank[:], wt_hi[:, q_, :], eb2[:, cols], True, False),
                            (bank[:], wt_lo[:, q_, :], eb2[:, cols], False, True)), *st_["wt", n], t_ebs, *fr)
            st_["mix", n] = t
            xs = X[b % 2][:, t_, cols]
            v = V("x2", lambda e: e.tensor_tensor(xs, xs, bank[:], ALU.add), t, st_["xa", b, t_])
            freed[i] = (v,)
            if c == 3:
                st_["out", b, t_] = load(f"out{t_}", ov[b, t_], X[b % 2][:, t_, :], v)
                if b + 2 < NB:
                    xin.setdefault(b + 2, []).append(
                        load(f"x{b % 2}_{t_}", X[b % 2][:, t_, :], xv[b + 2, t_], st_["out", b, t_]))

        def ffn_plan(b):
            plan = {}

            def at(t, f, *a):
                plan.setdefault(t, []).append((f, a))

            at(4, stats2, b, 3)
            at(4, norm2, b)
            for j in range(2):
                t0 = 5 + 5 * j
                for c in range(NU):
                    at(t0 + c // 2, route, b, j, c)
                    at(t0 + c // 2, route_t, b, j, c)
                    at(t0 + c // 2, route_r, b, j, c)
                at(t0 + 4, choose, b, j)
                at(t0 + 5, spread, b, j)
                for k in range(8):
                    at(t0 + 6 + k // 2, mix, b, j, k // 4, k % 4)
            return plan

        def ln1_plan(b):
            return {20: [(0, r) for r in range(4)], 21: [(1, r) for r in range(4)],
                    23: [(2, r) for r in range(4)], 24: [(3, r) for r in range(4)]}

        for p in range(3):
            load_ctx(p)
        load_mask(0)
        normalise(0)
        queries(0)
        keys(0)
        values(0)
        values(1)
        load_ctx(3)
        load_ctx(4)
        load_mask(1)

        TU = NB * NU
        ffn = {b: ffn_plan(b) for b in range(NB)}
        for s in range(4 * TU + 24):
            u, k = divmod(s, 4)
            b, t = divmod(s, 4 * NU)
            if s < 4 * TU:
                scores(s)
            if 1 <= s <= 4 * TU:
                turn_p(s - 1)
            if u + 1 < TU:
                if k == 0:
                    normalise(u + 1)
                    queries(u + 1)
                    if u + 2 < TU:
                        load_mask(u + 2) if u + 2 >= 2 else None
                if k == 1:
                    keys(u + 1)
                if k >= 2:
                    p = 2 * (u + 1) + k - 2
                    values(p)
                    if p + 3 < 2 * TU:
                        load_ctx(p + 3)
            if 1 <= s <= 4 * TU:
                weigh(s - 1)
            v = u - 1
            if 0 <= v < TU:
                if k == 1:
                    gelu(v)
                if k == 2:
                    turn_o(v)
                    project_out(v, 0)
                if k == 3:
                    project_out(v, 1)
                    if v % 2 and v % NU != NU - 1:
                        stats2(v // NU, (v % NU) // 2)
            if b >= 1:
                for f, a in ffn[b - 1].get(t, ()):
                    f(*a)
            elif b == NB and False:
                pass
            if b + 1 < NB and s < 4 * TU:
                if t == 16 and b + 1 < NB:
                    pass
                for tt, r in ln1_plan(b + 1).get(t, ()):
                    st_["s1"] = stats1(b + 1, tt, r, xin[b + 1][tt])
                if t == 26:
                    n1[b + 1] = norm1(b + 1, st_["s1"], n1[b])
                    free = (st_["WO", (b - 1) * NU + NU - 1],) if b else ()
                    rows_in[b + 1] = load_rows(b + 1, *free)

        Q.wait("sync", *[st_["out", NB - 1, t] for t in range(DT)])

        block = st.enter_context(nc.Block())

        @block.sync
        def _(e):
            Q.play("sync", e)

        @block.scalar
        def _(e):
            Q.play("scalar", e)

        @block.vector
        def _(e):
            Q.play("vector", e)

        @block.gpsimd
        def _(e):
            Q.play("gpsimd", e)

        @block.tensor
        def _(e):
            Q.play("tensor", e)


def kernel(x, ctx_4096, mask_Bx1x4096_ff1, g_xattn, g_ffn, L0_xattn_Wq, L0_xattn_bq, L0_xattn_Wk, L0_xattn_bk,
           L0_xattn_Wv, L0_xattn_bv, L0_xattn_Wo, L0_xattn_bo, L0_ffn_router_weight, L0_ffn_router_bias,
           L0_ffn_expert_bias):
    import numpy as np
    import concourse.bacc as bacc
    from concourse.bass_utils import run_bass_kernel_spmd

    def c(a):
        return np.ascontiguousarray(np.asarray(a))

    arrays = {
        "x": c(x), "ctx": c(ctx_4096), "mask": c(mask_Bx1x4096_ff1), "g_x": c(g_xattn), "g_f": c(g_ffn),
        "wqT": c(np.asarray(L0_xattn_Wq).T), "wkT": c(np.asarray(L0_xattn_Wk).T), "wvT": c(np.asarray(L0_xattn_Wv).T),
        "woT": c(np.asarray(L0_xattn_Wo).T),
        "bq": c(np.asarray(L0_xattn_bq).reshape(2, 128).T), "bk": c(np.asarray(L0_xattn_bk).reshape(2, 128).T),
        "bv": c(L0_xattn_bv), "bo": c(L0_xattn_bo),
        "wrT": c(np.asarray(L0_ffn_router_weight).T), "rb": c(L0_ffn_router_bias), "eb": c(L0_ffn_expert_bias),
    }
    nc = bacc.Bacc("TRN2", target_bir_lowering=False, num_devices=1, dynamic_dma_scratch_size=1024)
    args = [nc.dram_tensor("in_" + n, a.shape, mybir.dt.from_np(a.dtype), kind="ExternalInput").ap()
            for n, a in arrays.items()]
    args.append(nc.dram_tensor("out_y", (NB, D, S), F32, kind="ExternalOutput").ap())
    gated_block_kernel(nc, *args)
    r = run_bass_kernel_spmd(nc, [{"in_" + n: a for n, a in arrays.items()}], core_ids=[0])
    return r.results[0]["out_y"]
```

```python
from contextlib import ExitStack

import concourse.bass as bass
from concourse import mybir

F32 = mybir.dt.float32
F32R = mybir.dt.float32r
BF16 = mybir.dt.bfloat16
F16 = mybir.dt.float16
ALU = mybir.AluOpType
ACT = mybir.ActivationFunctionType
AX = mybir.AxisListType

NB, D, S = 8, 512, 2048
DT = D // 128
E = 256
H, DH = 8, 32
W = 128
U = 256
NU = S // U
SB = S // 128
NX = 64
EPS = 1e-5
SHIFT = 9.0
BIG = 1e9
QSCALE = 1.0 / float(DH) ** 0.5


def bf16_parts(v):
    import numpy as np
    parts, rest = [], np.float32(v)
    for _ in range(3):
        bits = np.array([rest], np.float32).view(np.uint32)
        bits = (bits + 0x7FFF + ((bits >> 16) & 1)) & np.uint32(0xFFFF0000)
        p = bits.view(np.float32)[0]
        parts.append(float(p))
        rest = np.float32(rest - p)
    return parts


SLOTS = dict(z32=-21.5, z_hi=-19, z_lo=-19, q=-16.75, q_hi=-12, q_lo=-11.25, k=-12.75, k32=-11, k_hi=-10.25, k_lo=-9.75, mk=-16.5, mkb=-13.75, rows=-12.5, v=-9.5, v32=-7.5, v1=-4.5, vr=-3.75, v2=-2.75, v3=-2.5, S=-0.25, top=1, exp=4.25, PT=4.75, pt_hi=5.5, pt_lo=6.75, PV=9.25, on=10.25, gelu=40.25, g2=41.5, OT=42, ot_hi=42.5, ot_lo=45.25, WO=46.75, x1=47.5, WO_gap=2.5, bn2=53, norm2=29.5, R0=31, R_gap=18, h=-1.25, hT=2.5, ht_hi=3.5, ht_lo=4.5, R=5.5, L=4.25, LT=6, c_top=7.5, c_exp=9, c_w=9, wT=10.25, wt_hi=13.25, wt_lo=13.5, xa=11, mix=14, x2=14.75, bn1=74.25, norm1=105.5)


SIDE = dict(z_lo="gpsimd", k_lo="gpsimd", vr="gpsimd", v3="gpsimd")


class Queues:

    def __init__(self, make):
        self.make, self.sems, self.count = make, {}, {}
        self.list = {e: [] for e in ("sync", "scalar", "vector", "gpsimd", "tensor")}
        self.seen = {e: {} for e in self.list}

    def op(self, eng, sem, fn, *waits, inc=1):
        if sem not in self.sems:
            self.sems[sem], self.count[sem] = self.make(sem), 0
        for name, n in waits:
            if self.seen[eng].get(name, 0) < n:
                self.seen[eng][name] = n
                self.list[eng].append(("wait", name, n))
        self.count[sem] += inc
        self.list[eng].append(("do", fn, sem, inc))
        return sem, self.count[sem]

    def wait(self, eng, *waits):
        for name, n in waits:
            if self.seen[eng].get(name, 0) < n:
                self.seen[eng][name] = n
                self.list[eng].append(("wait", name, n))

    def play(self, eng, e):
        for it in self.list[eng]:
            if it[0] == "wait":
                e.wait_ge(self.sems[it[1]], it[2])
            else:
                it[1](e).then_inc(self.sems[it[2]], it[3])


def gated_block_kernel(nc, x, ctx, mask, g_x, g_f, wqT, wkT, wvT, woT, bq, bk, bv, bo, wrT, rb, eb, out):
    with ExitStack() as st:
        def sb(name, shape, dt=F32):
            return st.enter_context(nc.sbuf_tensor(name, shape, dt))

        def pb(name):
            return st.enter_context(nc.psum_tensor(name, [128, 512], F32))

        Q = Queues(lambda n: st.enter_context(nc.semaphore("s_" + n)))
        op = Q.op

        X = [sb(f"X{i}", [128, DT, S]) for i in range(2)]
        wqk_hi = sb("wqk_hi", [128, DT, 2 * E], F32R)
        wqk_lo = sb("wqk_lo", [128, DT, 2 * E], F32R)
        wv = sb("wv", [128, DT, E])
        wo_hi = sb("wo_hi", [128, 2, D], F32R)
        wo_lo = sb("wo_lo", [128, 2, D], F32R)
        wr2 = sb("wr2", [128, SB, 2 * NX], F32R)
        eb2 = sb("eb2", [128, S], F32R)
        kz_hi = [sb(f"kz_hi{i}", [128, 2, 4, U], F32R) for i in range(2)]
        kz_lo = [sb(f"kz_lo{i}", [128, 2, 4, U], F32R) for i in range(2)]
        z32 = sb("z32", [128, DT, U])
        z_hi = sb("z_hi", [128, DT, U], F32R)
        z_lo = sb("z_lo", [128, DT, U], F32R)
        cx = [sb(f"cx{i}", [128, DT, W]) for i in range(3)]
        q_hi = [sb(f"q_hi{i}", [128, 2, U], F32R) for i in range(2)]
        q_lo = [sb(f"q_lo{i}", [128, 2, U], F32R) for i in range(2)]
        k32 = sb("k32", [128, 2, U])
        k_hi = sb("k_hi", [128, 2, U], F32R)
        k_lo = sb("k_lo", [128, 2, U], F32R)
        NP = 2
        P32 = [sb(f"P32_{i}", [128, 4, W]) for i in range(NP)]
        pt_hi = [sb(f"pt_hi{i}", [128, 4, W], F16) for i in range(2)]
        pt_lo = [sb(f"pt_lo{i}", [128, 4, W], F16) for i in range(2)]
        NV = 3
        NRW = 5
        LATER = -6
        v32 = sb("v32", [128, H, DH])
        vp = [[sb(f"v{k}_{i}", [128, H, DH + 1], BF16) for k in range(3)] for i in range(NV)]
        oo = [sb(f"oo{i}", [128, 2, 2, E]) for i in range(2)]
        o32 = [oo[i // 2][:, i % 2, :, :] for i in range(4)]
        ot_hi = sb("ot_hi", [128, 2, U], F32R)
        ot_lo = sb("ot_lo", [128, 2, U], F32R)
        hc = [sb(f"hc{i}", [128, 2, U]) for i in range(2)]
        ht_hi = sb("ht_hi", [128, 2, U], F32R)
        ht_lo = sb("ht_lo", [128, 2, U], F32R)
        rows = [sb(f"rows{i}", [128, U], BF16) for i in range(NRW)]
        mk = [sb(f"mk{i}", [128, U]) for i in range(2)]
        ident = sb("ident", [128, 128])
        id2 = sb("id2", [128, NX])
        ones3 = sb("ones3", [128, 128], BF16)
        bo6 = sb("bo6", [128, D], BF16)
        cst = sb("cst", [128, 24])
        bvb = sb("bvb", [128, E])
        rbb = sb("rbb", [128, NX])
        tgm = sb("tgm", [128, 128])
        bnst = sb("bnst", [128, DT, 4, 6])
        mv = sb("mv", [128, DT, 2])
        bn2 = sb("bn2", [128, DT, 4, 6])
        mv2 = sb("mv2", [128, DT, 2])
        ln1 = [sb(f"ln1_{i}", [128, 3, DT]) for i in range(2)]
        ln2 = sb("ln2", [128, 3, DT])
        mx = sb("mx", [128, 4, 4])
        rc = sb("rc", [128, 2, H])
        L = sb("L", [128, U])
        lg = sb("lg", [128, 2, NX])
        lr = sb("lr", [128, 2, NX])
        ex = sb("ex", [128, 2, NX])
        w2 = sb("w2", [128, 2, 2 * NX])
        t8 = sb("t8", [128, 2, 8])
        sc = sb("sc", [128, 2, 8])
        wt_hi = sb("wt_hi", [128, 2, 128], F32R)
        wt_lo = sb("wt_lo", [128, 2, 128], F32R)
        half = sb("half", [128, DT])

        NR = 6
        ring = [pb(f"ring{i}") for i in range(NR)]
        idle = [(i, ()) for i in range(NR)]
        PO = pb("PO")
        PR = pb("PR")

        def take():
            assert idle, "no bank: its readers are queued too late"
            i, w = idle.pop(0)
            return i, ring[i], w

        def give(i, *readers):
            idle.append((i, readers))

        def mm(*parts):
            def fn(e):
                for o, a, b, s0, s1 in parts:
                    last = e.matmul(o, a, b, start=s0, stop=s1)
                return last
            return fn

        def tr(*parts):
            def fn(e):
                for o, a, i in parts:
                    last = e.transpose(o, a, i)
                return last
            return fn

        def f32(ap):
            return ap.bitcast(F32)

        BQ, BK, TG, TF, SH, M05 = 0, 2, 4, 5, 6, 7

        stage = X[1]
        wst = stage[:, 0, :].rearrange("p (k n) -> p k n", k=DT)

        def load(sem, dst, src, *waits):
            return op("sync", sem, lambda e: e.dma_start(dst, src), *waits, inc=16)

        xv = x.rearrange("b (t p) s -> b t p s", p=128)
        ov = out.rearrange("b (t p) s -> b t p s", p=128)
        cv = ctx.rearrange("b (t p) s -> b p t s", p=128)
        mflat = mask.rearrange("b o s -> (b o) s")

        def G(sem, fn, *w):
            return op("gpsimd", sem, fn, *w)

        def V(sem, fn, *w):
            return op("vector", sem, fn, *w)

        def A(sem, fn, *w):
            return op("scalar", sem, fn, *w)

        def Z(sem, fn, *w):
            return op(SIDE[sem], sem, fn, *w)

        def T(sem, fn, *w):
            return op("tensor", sem, fn, *w)

        st_ = {}

        def load_ctx(p):
            b, w = divmod(p, S // W)
            i = p % 3
            free = (st_["v", p - 3],) if p >= 3 else ()
            st_["cx", p] = load(f"cx{i}", cx[i][:], cv[b][:, :, w * W:(w + 1) * W], *free)

        def load_mask(u):
            b, c = divmod(u, NU)
            i = u % 2
            free = (st_["k32", u - 2],) if u >= 2 else ()
            st_["mkl", u] = load(f"mk{i}", mk[i][:], mflat[b:b + 1, c * U:(c + 1) * U].to_broadcast([128, U]), *free)

        def mask_bits(u):
            i = u % 2
            st_["mk", u] = G("mk01", lambda e: e.tensor_scalar(mk[i][:], mk[i][:], 0.0, None, ALU.is_gt), st_["mkl", u])

        load("w_x", cst[:, TG:TG + 1], g_x[None, :].to_broadcast([128, 1]))
        load("w_x", cst[:, TF:TF + 1], g_f[None, :].to_broadcast([128, 1]))
        load("w_x", cst[:, BQ:BQ + 2], bq)
        t_small = load("w_x", cst[:, BK:BK + 2], bk)
        x_in = [[load(f"x0_{t}", X[0][:, t, :], xv[0, t]) for t in range(DT)]]
        for u in range(2):
            load_mask(u)
        load("w_qk", wst[:, :, 0:E], wqT.rearrange("(k p) n -> p k n", p=128))
        t_qk = load("w_qk", wst[:, :, E:2 * E], wkT.rearrange("(k p) n -> p k n", p=128))
        t_wv = load("w_v", wv[:], wvT.rearrange("(k p) n -> p k n", p=128))
        t_bv = load("w_v", bvb[:], bv[None, :].to_broadcast([128, E]))
        mT = stage[:, 1, 0:128]
        t_mT = load("w_mT", mT, mflat.rearrange("b (w i) -> (b w) i", i=128))
        mneg = stage[:, 1, 640:768]
        for p in range(3):
            load_ctx(p)
        wost = stage[:, 1, 1024:2048].rearrange("p (k n) -> p k n", k=2)
        t_wo = load("w_o", wost, woT.rearrange("(k p) n -> p k n", p=128))
        bost = hc[0][0:6].rearrange("p a n -> p (a n)")
        t_bo = load("w_bo", bost, bo[None, :].to_broadcast([6, D]))
        t_rb = load("w_rb", rbb[:], rb[None, :].to_broadcast([128, NX]))
        wrst = stage[:, 3, 0:1024].rearrange("p (k n) -> p k n", k=SB)
        t_wr = load("w_r", wrst, wrT.rearrange("(k p) n -> p k n", p=128))
        ebst = stage[:, 2, :]
        load("w_eb", ebst[0:NX, :], eb)
        t_eb = load("w_eb", ebst[NX:128, :], eb)

        a = G("g_set", lambda e: e.memset(ident[:], 0.0))
        t_id = G("g_set", lambda e: e.affine_select(out=ident[:], in_=ident[:], compare_op=ALU.not_equal, fill=1.0,
                                                   base=0, pattern=[[-1, 128]], channel_multiplier=1), a)
        b = G("g_set", lambda e: e.memset(id2[:], 0.0))
        b = G("g_set", lambda e: e.affine_select(out=id2[:], in_=id2[:], compare_op=ALU.not_equal, fill=1.0,
                                                 base=0, pattern=[[-1, NX]], channel_multiplier=1), b)
        t_id2 = G("g_set", lambda e: e.affine_select(out=id2[:], in_=id2[:], compare_op=ALU.not_equal, fill=1.0,
                                                     base=-NX, pattern=[[-1, NX]], channel_multiplier=1), b)
        G("g_set", lambda e: e.memset(half[:], -0.5))
        t_cst = G("g_set", lambda e: e.memset(cst[:, SH:SH + 1], SHIFT))
        t_vone = [G("g_set", lambda e, i=i, k=k: e.memset(vp[i][k][:, :, DH:DH + 1], 1.0 if k == 0 else 0.0))
                  for i in range(NV) for k in range(3)][-1]
        a = V("v_set", lambda e: e.memset(ones3[:], 1.0))
        bz = V("v_set", lambda e: e.memset(bo6[:], 0.0))
        for i in range(NRW):
            t_rz = V("v_set", lambda e, i=i: e.memset(rows[i][:], 0.0))
        a = G("g_set", lambda e: e.affine_select(out=ones3[:], in_=ones3[:], compare_op=ALU.is_ge, fill=0.0,
                                                 base=-6, pattern=[[0, 128]], channel_multiplier=1), a)
        t_ones3 = G("g_set", lambda e: e.affine_select(out=ones3[:], in_=ones3[:], compare_op=ALU.is_ge, fill=0.0,
                                                       base=8, pattern=[[0, 128]], channel_multiplier=-1), a)

        for i in range(2):
            G("g_kz", lambda e, i=i: e.memset(f32(kz_hi[i][:]), 0.0))
            t_kz0 = G("g_kz", lambda e, i=i: e.memset(f32(kz_lo[i][:]), 0.0))

        t_tg = A("a_set", lambda e: e.activation(cst[:, TG:TG + 2], cst[:, TG:TG + 2], ACT.Tanh), t_small)
        t_bq = V("v_set", lambda e: e.tensor_scalar(cst[:, BQ:BQ + 2], cst[:, BQ:BQ + 2], QSCALE, None, ALU.mult), t_small)

        def stats1(b, t, r, xin):
            return V("bn1", lambda e: e.bn_stats(bnst[:, t, r, :], X[b % 2][:, t, r * 512:(r + 1) * 512]), xin)

        def norm1(b, last, free):
            l = ln1[b % 2]
            for t in range(DT):
                v = V("bn1a", lambda e, t=t: e.bn_aggr(mv[:, t, :], bnst[:, t, :, :].rearrange("p a c -> p (a c)")), last, free)
            V("bn1b", lambda e: e.tensor_scalar(l[:, 0, :], mv[:, :, 0], -1.0, None, ALU.mult), v)
            v = V("bn1b", lambda e: e.tensor_scalar(l[:, 1, :], mv[:, :, 1], EPS, None, ALU.add))
            return G("rstd1", lambda e: e.tensor_tensor(l[:, 2, :], l[:, 1, :], half[:], ALU.pow), v)

        for t in range(DT):
            for r in range(4):
                last = stats1(0, t, r, x_in[0][t])
        n1 = {0: norm1(0, last, t_cst)}

        V("v_w", lambda e: e.tensor_scalar(wst[:, :, 0:E], wst[:, :, 0:E], QSCALE, None, ALU.mult), t_qk)
        a = V("v_w", lambda e: e.tensor_copy(wqk_hi[:, :, E:2 * E], wst[:, :, E:2 * E]))
        a = V("v_w", lambda e: e.tensor_copy(wqk_hi[:, :, 0:E], wst[:, :, 0:E]), a)
        t_wqk = V("v_w", lambda e: e.tensor_tensor(wqk_lo[:], wst, f32(wqk_hi[:]), ALU.subtract), a)
        tgr = stage[:, 1, 128:256]
        keep = stage[:, 1, 256:640].bitcast(BF16).rearrange("p (k i) -> p k i", k=6)
        rows_d = nc.dram_tensor("rows_d", (9, 128, 128), BF16, kind="Internal").ap()
        V("v_m", lambda e: e.tensor_scalar(tgr, mT, cst[:, TG:TG + 1], None, ALU.mult), t_mT, t_tg)
        a = V("v_m", lambda e: e.tensor_scalar(mneg, mT, 0.0, 1.0, ALU.is_gt, ALU.subtract))
        for k, part in enumerate(bf16_parts(BIG)):
            V("v_m", lambda e, k=k, part=part: e.tensor_scalar(keep[:, 3 + k, :], mneg, part, None, ALU.mult), a)
        a = V("v_m", lambda e: e.tensor_copy(keep[:, 0, :], tgr), a)
        a = V("v_m", lambda e: e.tensor_tensor(tgr, tgr, keep[:, 0, :], ALU.subtract), a)
        a = V("v_m", lambda e: e.tensor_copy(keep[:, 1, :], tgr), a)
        a = V("v_m", lambda e: e.tensor_tensor(keep[:, 2, :], tgr, keep[:, 1, :], ALU.subtract), a)
        for k0, src in ((0, keep[:, 0:2, :]), (2, keep[:, 0:3, :]), (5, keep[:, 0:1, :]), (6, keep[:, 3:6, :])):
            n = src.shape[1]
            t_keep = load("rows_d", rows_d[k0:k0 + n].rearrange("k p i -> p k i"), src, a)
        i, bank, w = take()
        a = T("setT", lambda e, bank=bank: e.transpose(bank[:, 0:128], mT, ident[:]), t_mT, t_id, *w)
        t_tgm = V("v_m", lambda e, bank=bank: e.tensor_scalar(tgm[:], bank[:, 0:128], cst[:, TG:TG + 1], None, ALU.mult), a, t_tg)
        give(i, t_tgm)
        def load_rows(u):
            free = (st_["WO", u - NRW, 1],) if u >= NRW else (t_keep, t_rz)
            st_["rows", u] = load(f"rows{u % NRW}", rows[u % NRW][0:9, :],
                                  rows_d[:, 2 * u:2 * u + 2, :].rearrange("k w i -> k (w i)"), *free)

        xin = {0: x_in[0]}

        def z_full(u):
            b, c = divmod(u, NU)
            l = ln1[b % 2]
            free = (st_["z_lo", u - 1],) if u else ()
            for t in range(DT):
                z = G("z32", lambda e, t=t: e.tensor_scalar(z32[:, t, :], X[b % 2][:, t, c * U:(c + 1) * U],
                                                            l[:, 0, t:t + 1], l[:, 2, t:t + 1], ALU.add, ALU.mult),
                      n1[b], *free)
            st_["z32", u] = z

        def z_high(u):
            free = (st_["qk", u - 1, 1, 1],) if u else ()
            st_["z_hi", u] = A("z_hi", lambda e: e.activation(z_hi[:], z32[:], ACT.Copy), st_["z32", u], *free)

        def z_low(u):
            free = (st_["qk", u - 1, 1, 1],) if u else ()
            st_["z_lo", u] = Z("z_lo", lambda e: e.tensor_tensor(z_lo[:], z32[:], f32(z_hi[:]), ALU.subtract),
                               st_["z_hi", u], *free)

        def project(u, kind, m):
            if m == 0:
                st_["qkb", u, kind] = take()
            i, bank, w = st_["qkb", u, kind]
            parts = []
            n = 0
            for t in range(DT):
                cols = slice(kind * E + m * 128, kind * E + (m + 1) * 128)
                for a_, z_ in ((wqk_hi, z_hi), (wqk_lo, z_hi), (wqk_hi, z_lo)):
                    parts.append((bank[:, m * U:(m + 1) * U], a_[:, t, cols], z_[:, t, :], n == 0, n == 3 * DT - 1))
                    n += 1
            st_["qk", u, kind, m] = T("qk", mm(*parts), st_["z_hi", u], st_["z_lo", u], t_wqk, *w)

        def q_high(u):
            i, bank, _ = st_["qkb", u, 0]
            free = (st_["S", 4 * (u - 2) + 3],) if u >= 2 else ()
            for m in range(2):
                st_["q_hi", u] = A("q_hi", lambda e, m=m: e.activation(
                    q_hi[u % 2][:, m, :], bank[:, m * U:(m + 1) * U], ACT.Identity, bias=cst[:, BQ + m:BQ + m + 1]),
                    st_["qk", u, 0, 1], t_bq, *free)

        def q_low(u):
            i, bank, _ = st_["qkb", u, 0]
            free = (st_["S", 4 * (u - 2) + 3],) if u >= 2 else ()
            for m in range(2):
                l = V("q_lo", lambda e, m=m: e.scalar_tensor_tensor(
                    out=q_lo[u % 2][:, m, :], in0=bank[:, m * U:(m + 1) * U], scalar=cst[:, BQ + m:BQ + m + 1],
                    in1=f32(q_hi[u % 2][:, m, :]), op0=ALU.add, op1=ALU.subtract), st_["q_hi", u], t_bq, *free)
            give(i, l)
            st_["q", u] = (st_["q_hi", u], l)

        def k_full(u):
            i, bank, _ = st_["qkb", u, 1]
            free = (st_["k_lo", u - 1],) if u else ()
            for m in range(2):
                v = V("k32", lambda e, m=m: e.scalar_tensor_tensor(
                    out=k32[:, m, :], in0=bank[:, m * U:(m + 1) * U], scalar=cst[:, BK + m:BK + m + 1], in1=mk[u % 2][:],
                    op0=ALU.add, op1=ALU.mult), st_["qk", u, 1, 1], st_["mk", u], *free)
            give(i, v)
            st_["k32", u] = v

        def k_spread(u, n, src, dst, tok):
            free = (st_["S", 4 * (u - 2) + 3],) if u >= 2 else (t_kz0,)
            for g in range(4):
                q = load(f"kz{u % 2}_{n}", f32(dst[32 * g:32 * g + 32, :, g, :]), f32(src[32 * g:32 * g + 32, :, :]),
                         tok, *free)
            st_["kz", u, n] = q

        def k_high(u):
            free = (st_["kz", u - 1, 0],) if u else ()
            h = A("k_hi", lambda e: e.activation(k_hi[:], k32[:], ACT.Copy), st_["k32", u], *free)
            st_["k_hi", u] = h
            k_spread(u, 0, k_hi, kz_hi[u % 2], h)

        def k_low(u):
            free = (st_["kz", u - 1, 1],) if u else ()
            l = Z("k_lo", lambda e: e.tensor_tensor(k_lo[:], k32[:], f32(k_hi[:]), ALU.subtract), st_["k_hi", u],
                  st_["k32", u], *free)
            st_["k_lo", u] = l
            k_spread(u, 1, k_lo, kz_lo[u % 2], l)

        def v_mm(p):
            i, bank, w = take()
            c = cx[p % 3]
            st_["v", p] = T("v", mm(*[(bank[:, 0:E], c[:, k, :], wv[:, k, :], k == 0, k == DT - 1) for k in range(DT)]),
                            st_["cx", p], t_wv, *w)
            st_["vb", p] = i, bank
            if p + 3 < 2 * TU:
                load_ctx(p + 3)

        def v_full(p):
            i, bank = st_["vb", p]
            prev = (st_["v3", p - 1],) if p else ()
            a = V("v32", lambda e: e.tensor_tensor(v32[:], bank[:, 0:E].rearrange("p (h d) -> p h d", h=H),
                                                   bvb[:].rearrange("p (h d) -> p h d", h=H), ALU.add),
                  st_["v", p], t_bv, *prev)
            give(i, a)
            st_["v32", p] = a

        def v_1(p):
            free = (st_["PV", 2 * (p - NV) + 1],) if p >= NV else (t_vone,)
            st_["v1", p] = A("v1", lambda e: e.activation(vp[p % NV][0][:, :, 0:DH], v32[:], ACT.Copy), st_["v32", p], *free)

        def v_r(p):
            st_["vr", p] = Z("vr", lambda e: e.tensor_tensor(v32[:], v32[:], vp[p % NV][0][:, :, 0:DH], ALU.subtract),
                             st_["v1", p], st_["v32", p])

        def v_2(p):
            st_["v2", p] = A("v2", lambda e: e.activation(vp[p % NV][1][:, :, 0:DH], v32[:], ACT.Copy), st_["vr", p])

        def v_3(p):
            st_["v3", p] = Z("v3", lambda e: e.tensor_tensor(vp[p % NV][2][:, :, 0:DH], v32[:], vp[p % NV][1][:, :, 0:DH],
                                                             ALU.subtract), st_["v2", p], st_["vr", p], st_["v1", p])

        def scores(s):
            u, k = divmod(s, 4)
            w, m = divmod(k, 2)
            i, bank, fr = take()
            cols = slice(w * W, (w + 1) * W)
            kh, kl = kz_hi[u % 2][:, m, :, cols], kz_lo[u % 2][:, m, :, cols]
            qh, ql = q_hi[u % 2][:, m, cols], q_lo[u % 2][:, m, cols]
            mrow = rows[u % NRW][:, cols].unsqueeze(1).to_broadcast([128, 4, W])
            o = bank[:].rearrange("p (h j) -> p h j", h=4)
            st_["S", s] = T("S", mm((o, ones3[:], mrow, True, False), (o, qh, kh, False, False),
                                    (o, ql, kh, False, False), (o, qh, kl, False, True)),
                            *st_["q", u], st_["kz", u, 0], st_["kz", u, 1], st_["rows", u], t_ones3, *fr)
            st_["Sb", s] = i, o

        def top(s):
            i, o = st_["Sb", s]
            m = mx[:, s % 4, :]
            v = V("mx", lambda e: e.tensor_reduce(m, o, AX.X, ALU.max), st_["S", s])
            free = (st_["PT", s - NP],) if s >= NP else ()
            v = V("sub", lambda e: e.tensor_tensor(P32[s % NP][:], o, m.unsqueeze(2).to_broadcast([128, 4, W]),
                                                   ALU.subtract), v, *free)
            give(i, v)
            st_["sub", s] = v

        def expo(s):
            P = P32[s % NP]
            st_["exp", s] = A("exp", lambda e: e.activation(P[:], P[:], ACT.Exp, bias=cst[:, SH:SH + 1]), st_["sub", s], t_cst)

        def turn_p(s):
            i, bank, fr = take()
            P = P32[s % NP]
            st_["PT", s] = T("PT", tr(*[(bank[:, h * W:(h + 1) * W], P[:, h, :], ident[:]) for h in range(4)]),
                             st_["exp", s], t_id, *fr)
            st_["PTb", s] = i, bank[:].rearrange("p (h j) -> p h j", h=4)

        def p_high(s):
            i, o = st_["PTb", s]
            free = (st_["PV", s - 2],) if s >= 2 else ()
            st_["pt_hi", s] = A("pt_hi", lambda e: e.activation(pt_hi[s % 2][:], o, ACT.Copy), st_["PT", s], *free)

        def p_low(s):
            i, o = st_["PTb", s]
            free = (st_["PV", s - 2],) if s >= 2 else ()
            l = V("pt_lo", lambda e: e.tensor_tensor(pt_lo[s % 2][:], o, pt_hi[s % 2][:], ALU.subtract),
                  st_["pt_hi", s], *free)
            give(i, l)
            st_["pt_lo", s] = l

        def weigh(s):
            u, k = divmod(s, 4)
            w, m = divmod(k, 2)
            p = 2 * u + w
            vv = vp[p % NV]
            ph, pl = pt_hi[s % 2], pt_lo[s % 2]
            parts = []
            for h in range(4):
                hh = 4 * m + h
                o = PO[:, hh * (DH + 1):(hh + 1) * (DH + 1)]
                for n, (a, k_) in enumerate(((ph, 0), (ph, 1), (ph, 2), (pl, 0), (pl, 1))):
                    parts.append((o, a[:, h, :], vv[k_][:, hh, :], n == 0, n == 4))
            free = (st_["on", p - 1],) if m == 0 and p else ()
            st_["PV", s] = T("PV", mm(*parts), st_["pt_hi", s], st_["pt_lo", s], st_["v1", p], st_["v2", p], st_["v3", p],
                             *free)

        def divide(p):
            o = PO[:, 0:H * (DH + 1)].rearrange("p (h d) -> p h d", h=H)
            u, w = divmod(p, 2)
            r = rc[:, p % 2, :].unsqueeze(2)
            v = V("rc", lambda e: e.reciprocal(r, o[:, :, DH:DH + 1]), st_["PV", 2 * p + 1])
            od = o32[u % 4][:, w, :].rearrange("p (h d) -> p h d", h=H)
            free = (st_["OT", u - 4],) if u >= 4 else ()
            st_["on", p] = V("on", lambda e: e.tensor_tensor(od, o[:, :, 0:DH], r.to_broadcast([128, H, DH]), ALU.mult),
                             v, *free)

        def gelu(u):
            o = oo[u // 2 % 2]
            st_["gelu", u] = st_["gelu", u + 1] = A("gelu", lambda e: e.activation(o[:], o[:], ACT.Gelu),
                                                    st_["on", 2 * u + 3])

        def scale_o(u):
            o = o32[u % 4]
            for w in range(2):
                p = 2 * u + w
                st_["g2", u] = G("g2", lambda e, w=w, p=p: e.tensor_scalar(o[:, w, :], o[:, w, :], tgm[:, p:p + 1], None,
                                                                          ALU.mult), st_["gelu", u], t_tgm)

        def turn_o(u):
            i, bank, fr = take()
            st_["OT", u] = T("OT", tr(*[(bank[:, m * U + w * W:m * U + (w + 1) * W],
                                         o32[u % 4][:, w, m * 128:(m + 1) * 128], ident[:])
                                        for m in range(2) for w in range(2)]), st_["g2", u], t_id, *fr)
            st_["OTb", u] = i, bank[:].rearrange("p (m i) -> p m i", m=2)

        def o_high(u):
            i, o = st_["OTb", u]
            free = (st_["WO", u - 1, 1],) if u else ()
            st_["ot_hi", u] = A("ot_hi", lambda e: e.activation(ot_hi[:], o, ACT.Copy), st_["OT", u], *free)

        def o_low(u):
            i, o = st_["OTb", u]
            free = (st_["WO", u - 1, 1],) if u else ()
            l = V("ot_lo", lambda e: e.tensor_tensor(ot_lo[:], o, f32(ot_hi[:]), ALU.subtract), st_["ot_hi", u], *free)
            give(i, l)
            st_["ot_lo", u] = l

        def project_out(u, j):
            b, c = divmod(u, NU)
            i, bank, fr = take()
            parts = []
            for n in range(2):
                t = 2 * j + n
                o = bank[:, n * U:(n + 1) * U]
                cols = slice(t * 128, (t + 1) * 128)
                parts.append((o, bo6[:, cols], rows[u % NRW][:], True, False))
                for m in range(2):
                    for q_, (a, z) in enumerate(((wo_hi, ot_hi), (wo_lo, ot_hi), (wo_hi, ot_lo))):
                        parts.append((o, a[:, m, cols], z[:, m, :], False, m == 1 and q_ == 2))
            st_["WO", u, j] = T("WO", mm(*parts), st_["ot_hi", u], st_["ot_lo", u], st_["rows", u], t_bo6, t_wos, *fr)
            st_["WOb", u, j] = i, bank[:].rearrange("p (n i) -> p n i", n=2)

        def add_x(u, j):
            b, c = divmod(u, NU)
            i, o = st_["WOb", u, j]
            xs = X[b % 2][:, 2 * j:2 * j + 2, c * U:(c + 1) * U]
            v = V("x1", lambda e: e.tensor_tensor(xs, xs, o, ALU.add), st_["WO", u, j])
            give(i, v)
            st_["x1", u, j] = v

        def stats2(b, r):
            for t in range(DT):
                st_["bn2", b, r] = V("bn2", lambda e, t=t: e.bn_stats(bn2[:, t, r, :], X[b % 2][:, t, r * 512:(r + 1) * 512]),
                                  st_["x1", b * NU + 2 * r, 1], st_["x1", b * NU + 2 * r + 1, 1], *((st_["mv2", b - 1],) if b else ()))

        def norm2(b):
            for t in range(DT):
                v = V("mv2", lambda e, t=t: e.bn_aggr(mv2[:, t, :], bn2[:, t, :, :].rearrange("p a c -> p (a c)")),
                      *[st_["bn2", b, r] for r in range(4)])
            st_["mv2", b] = v
            free = (st_["ac", b - 1, 1],) if b else ()
            V("ln2", lambda e: e.tensor_scalar(ln2[:, 0, :], mv2[:, :, 0], -1.0, None, ALU.mult), v, *free)
            v = V("ln2", lambda e: e.tensor_scalar(ln2[:, 1, :], mv2[:, :, 1], EPS, None, ALU.add))
            st_["ln2", b] = G("rstd2", lambda e: e.tensor_tensor(ln2[:, 2, :], ln2[:, 1, :], half[:], ALU.pow), v)

        def r_full(b, j, c):
            n = (b * 2 + j) * NU + c
            free = (st_["hT", n - 2],) if n >= 2 else (t_bos,)
            for q_ in range(2):
                t = 2 * j + q_
                st_["h", n] = G("h", lambda e, q_=q_, t=t: e.tensor_scalar(
                    hc[n % 2][:, q_, :], X[b % 2][:, t, c * U:(c + 1) * U], ln2[:, 0, t:t + 1], ln2[:, 2, t:t + 1],
                    ALU.add, ALU.mult), st_["ln2", b], *free)

        def r_turn(b, j, c):
            n = (b * 2 + j) * NU + c
            i, bank, fr = take()
            st_["hT", n] = T("hT", tr(*[(bank[:, a * U + q_ * 128:a * U + (q_ + 1) * 128],
                                         hc[n % 2][:, q_, a * 128:(a + 1) * 128], ident[:])
                                        for a in range(2) for q_ in range(2)]), st_["h", n], t_id, *fr)
            st_["hTb", n] = i, bank[:].rearrange("p (a i) -> p a i", a=2)

        def r_high(b, j, c):
            n = (b * 2 + j) * NU + c
            i, o = st_["hTb", n]
            free = (st_["R", n - 1],) if n else ()
            st_["ht_hi", n] = A("ht_hi", lambda e: e.activation(ht_hi[:], o, ACT.Copy), st_["hT", n], *free)

        def r_low(b, j, c):
            n = (b * 2 + j) * NU + c
            i, o = st_["hTb", n]
            free = (st_["R", n - 1],) if n else ()
            l = V("ht_lo", lambda e: e.tensor_tensor(ht_lo[:], o, f32(ht_hi[:]), ALU.subtract), st_["ht_hi", n], *free)
            give(i, l)
            st_["ht_lo", n] = l

        def r_mm(b, j, c):
            n = (b * 2 + j) * NU + c
            parts = []
            for a in range(2):
                for q_, z in enumerate((ht_hi, ht_lo)):
                    parts.append((PR[:, 0:U], wr2[:, 2 * c + a, :], z[:, a, :], c == 0 and a == 0 and q_ == 0,
                                  c == NU - 1 and a == 1 and q_ == 1))
            free = (st_["L", b * 2 + j - 1],) if c == 0 and n else ()
            st_["R", n] = T("R", mm(*parts), st_["ht_hi", n], st_["ht_lo", n], t_wrs, *free)

        def c_logits(b, j):
            n = b * 2 + j
            free = (st_["LT", n - 1],) if n else ()
            st_["L", n] = A("L", lambda e: e.activation(L[:], PR[:, 0:U], ACT.Copy), st_["R", n * NU + NU - 1], *free)

        def c_turn(b, j):
            n = b * 2 + j
            i, bank, fr = take()
            st_["LT", n] = T("LT", mm(*[(bank[:, q_ * NX:(q_ + 1) * NX], L[:, q_ * 128:(q_ + 1) * 128], id2[:], True, True)
                                        for q_ in range(2)]), st_["L", n], t_id2, *fr)
            st_["LTb", n] = i, bank[:, 0:2 * NX].rearrange("p (q x) -> p q x", q=2)

        def c_top(b, j):
            n = b * 2 + j
            i, o = st_["LTb", n]
            free = (st_["w2", n - 1],) if n else ()
            v = V("lg", lambda e: e.tensor_tensor(lg[:], o, rbb[:].unsqueeze(1).to_broadcast([128, 2, NX]), ALU.add),
                  st_["LT", n], t_rb, *free)
            give(i, v)
            for q_ in range(2):
                v1 = V("top", lambda e, q_=q_: e.max(t8[:, q_, :], lg[:, q_, :]), v)
            v2 = V("neg", lambda e: e.tensor_scalar(sc[:, :, 0:1], t8[:, :, 0:1], -1.0, None, ALU.mult), v1, *(
                (st_["xa", b - 1 if j == 0 else b, 3 if j == 0 else 1],) if n else ()))
            st_["neg", n] = v2
            for q_ in range(2):
                v3 = V("top", lambda e, q_=q_: e.match_replace(lr[:, q_, :], t8[:, q_, :], lg[:, q_, :], -3.0e38), v1)
            st_["sel", n] = V("top", lambda e: e.tensor_tensor(lr[:], lr[:], lg[:], ALU.not_equal), v3)

        def c_exp(b, j):
            n = b * 2 + j
            for q_ in range(2):
                st_["ex", n] = A("ex", lambda e, q_=q_: e.activation(ex[:, q_, :], lg[:, q_, :], ACT.Exp,
                                                                     bias=sc[:, q_, 0:1], accum_out=sc[:, q_, 1:2]),
                                 st_["neg", n], *((st_["w2", n - 1],) if n else ()))

        def c_weights(b, j):
            n = b * 2 + j
            free = (st_["wT", n - 1],) if n else ()
            v3 = V("top", lambda e: e.tensor_tensor(ex[:], ex[:], lr[:], ALU.mult), st_["ex", n], st_["sel", n])
            v4 = V("top", lambda e: e.reciprocal(sc[:, :, 3:4], sc[:, :, 1:2]))
            v3 = V("top", lambda e: e.tensor_reduce(sc[:, :, 2:3], ex[:], AX.X, ALU.add), v3)
            v4 = V("top", lambda e: e.tensor_scalar(sc[:, :, 4:5], sc[:, :, 3:4], cst[:, TF:TF + 1], None, ALU.mult), v4, t_tg)
            for q_ in range(2):
                v5 = V("w2", lambda e, q_=q_: e.tensor_scalar(
                    w2[:, q_, :].rearrange("p (a x) -> p a x", a=2), ex[:, q_, :].unsqueeze(1).to_broadcast([128, 2, NX]),
                    sc[:, q_, 4:5], None, ALU.mult), v3, v4, *free)
            st_["w2", n] = v5
            v6 = V("top", lambda e: e.tensor_tensor(sc[:, :, 5:6], sc[:, :, 2:3], sc[:, :, 4:5], ALU.mult), v3, v4)
            v6 = V("top", lambda e: e.tensor_tensor(sc[:, :, 5:6], sc[:, :, 5:6], ln2[:, 2, 2 * j:2 * j + 2].unsqueeze(2),
                                                    ALU.mult), v6, st_["ln2", b])
            V("top", lambda e: e.tensor_scalar(sc[:, :, 6:7], sc[:, :, 5:6], 1.0, None, ALU.add), v6)
            st_["ac", b, j] = V("top", lambda e: e.tensor_tensor(sc[:, :, 7:8], sc[:, :, 5:6],
                                                                 ln2[:, 0, 2 * j:2 * j + 2].unsqueeze(2), ALU.mult), v6)

        def w_turn(b, j):
            n = b * 2 + j
            i, bank, fr = take()
            st_["wT", n] = T("wT", tr(*[(bank[:, q_ * 128:(q_ + 1) * 128], w2[:, q_, :], ident[:]) for q_ in range(2)]),
                             st_["w2", n], t_id, *fr)
            st_["wTb", n] = i, bank[:, 0:256].rearrange("p (q t) -> p q t", q=2)

        def w_high(b, j):
            n = b * 2 + j
            i, o = st_["wTb", n]
            free = (st_["mix", n - 1],) if n else ()
            st_["wt_hi", n] = A("wt_hi", lambda e: e.activation(wt_hi[:], o, ACT.Copy), st_["wT", n], *free)

        def w_low(b, j):
            n = b * 2 + j
            i, o = st_["wTb", n]
            free = (st_["mix", n - 1],) if n else ()
            l = V("wt_lo", lambda e: e.tensor_tensor(wt_lo[:], o, f32(wt_hi[:]), ALU.subtract), st_["wt_hi", n], *free)
            give(i, l)
            st_["wt_lo", n] = l

        def scale_x(b, t):
            j, q_ = divmod(t, 2)
            xs = X[b % 2][:, t, :]
            st_["xa", b, t] = G("xa", lambda e: e.tensor_scalar(xs, xs, sc[:, q_, 6:7], sc[:, q_, 7:8], ALU.mult, ALU.add),
                                st_["ac", b, j], st_["h", (b * 2 + j) * NU + NU - 1])

        def mix(b, t, c):
            n, q_ = b * 2 + t // 2, t % 2
            i, bank, fr = take()
            cols = slice(c * 512, (c + 1) * 512)
            st_["mix", n] = T("mix", mm((bank[:], wt_hi[:, q_, :], eb2[:, cols], True, False),
                                        (bank[:], wt_lo[:, q_, :], eb2[:, cols], False, True)),
                              st_["wt_hi", n], st_["wt_lo", n], t_ebs, *fr)
            st_["mixb", b, t, c] = i, bank, st_["mix", n]

        def add_mix(b, t, c):
            i, bank, tok = st_["mixb", b, t, c]
            xs = X[b % 2][:, t, c * 512:(c + 1) * 512]
            v = V("x2", lambda e: e.tensor_tensor(xs, xs, bank[:], ALU.add), tok, st_["xa", b, t])
            give(i, v)
            if c == 3:
                st_["out", b, t] = load(f"out{t}", ov[b, t], X[b % 2][:, t, :], v)
                if b + 2 < NB:
                    xin.setdefault(b + 2, []).append(
                        load(f"x{b % 2}_{t}", X[b % 2][:, t, :], xv[b + 2, t], st_["out", b, t]))

        def input_stats(b, t, r):
            st_["s1", b, t, r] = stats1(b, t, r, xin[b][t])

        def input_norm(b):
            n1[b] = norm1(b, [st_["s1", b, t, r] for t in range(DT) for r in range(4)][-1], n1[b - 1])

        TU = NB * NU
        plan = []

        def at(slot, fn, *args, late=0):
            plan.append((slot, late, len(plan), fn, args))

        C = SLOTS
        for u in range(TU):
            o = 16 * u
            at(o + C["rows"], load_rows, u)
            at(o + C["z32"], z_full, u)
            at(o + C["z_hi"], z_high, u)
            at(o + C["z_lo"], z_low, u)
            for m in range(2):
                at(o + C["q"] + m, project, u, 0, m)
                at(o + C["k"] + m, project, u, 1, m)
            at(o + C["q_hi"], q_high, u)
            at(o + C["q_lo"], q_low, u)
            at(o + C["k32"], k_full, u)
            at(o + C["k_hi"], k_high, u)
            at(o + C["k_lo"], k_low, u)
            if u >= 2:
                at(o + C["mk"], load_mask, u)
            at(o + C["mkb"], mask_bits, u)
            for w in range(2):
                p = 2 * u + w
                for n, (d, f) in enumerate((("v", v_mm), ("v32", v_full), ("v1", v_1), ("vr", v_r), ("v2", v_2), ("v3", v_3))):
                    at(o + 8 * w + C[d], f, p)
                at(o + 8 * w + 4 + C["on"], divide, p)
            for k in range(4):
                s = 4 * u + k
                for d, f in (("S", scores), ("top", top), ("exp", expo), ("PT", turn_p), ("pt_hi", p_high),
                             ("pt_lo", p_low), ("PV", weigh)):
                    at(o + 4 * k + C[d], f, s)
            if u % 2 == 0:
                at(o + C["gelu"], gelu, u)
            if u % 2:
                o -= 8
            for d, f in (("g2", scale_o), ("OT", turn_o), ("ot_hi", o_high), ("ot_lo", o_low)):
                at(o + C[d], f, u)
            for j in range(2):
                at(o + C["WO"] + C["WO_gap"] * j, project_out, u, j)
                at(o + C["x1"] + C["WO_gap"] * j, add_x, u, j)
            if u % 2:
                at(o + C["bn2"], stats2, u // NU, (u % NU) // 2)
        for b in range(NB):
            o = 128 * (b + 1)
            at(o + C["norm2"], norm2, b)
            for j in range(2):
                q = o + C["R0"] + C["R_gap"] * j
                for c in range(NU):
                    for d, f in (("h", r_full), ("hT", r_turn), ("ht_hi", r_high), ("ht_lo", r_low), ("R", r_mm)):
                        at(q + 2 * c + C[d], f, b, j, c)
                q += 16
                for d, f in (("L", c_logits), ("LT", c_turn), ("c_top", c_top), ("c_exp", c_exp), ("c_w", c_weights),
                             ("wT", w_turn), ("wt_hi", w_high), ("wt_lo", w_low)):
                    at(q + C[d], f, b, j)
                for q_ in range(2):
                    at(q + C["xa"] + 3 * q_, scale_x, b, 2 * j + q_)
                    for c in range(4):
                        at(q + C["mix"] + 4 * q_ + c, mix, b, 2 * j + q_, c)
                        at(q + C["x2"] + 4 * q_ + c, add_mix, b, 2 * j + q_, c)
            if b:
                o = 128 * (b - 1)
                for t in range(DT):
                    for r in range(4):
                        at(o + C["bn1"] + 8 * t + 2 * r, input_stats, b, t, r)
                at(o + C["norm1"], input_norm, b)

        todo = sorted(plan, key=lambda x: x[:3])
        first = [x for x in todo if x[0] < LATER]
        for slot, late, n, fn, args in first:
            fn(*args)

        a = A("a_w", lambda e: e.activation(wo_hi[:], wost, ACT.Copy), t_wo)
        t_wos = V("v_w", lambda e: e.tensor_tensor(wo_lo[:], wost, f32(wo_hi[:]), ALU.subtract), a)
        a = A("a_w", lambda e: e.activation(wr2[:, :, 0:NX], wrst, ACT.Copy), t_wr)
        t_wrs = V("v_w", lambda e: e.tensor_tensor(wr2[:, :, NX:2 * NX], wrst, f32(wr2[:, :, 0:NX]), ALU.subtract), a)
        bp = [stage[0:6, 3, 1024 + 256 * k:1280 + 256 * k].bitcast(BF16) for k in range(3)]
        a = V("v_w", lambda e: e.tensor_copy(bp[0], bost), t_bo)
        a = V("v_w", lambda e: e.tensor_tensor(bost, bost, bp[0], ALU.subtract), a)
        a = V("v_w", lambda e: e.tensor_copy(bp[1], bost), a)
        t_bos = a = V("v_w", lambda e: e.tensor_tensor(bp[2], bost, bp[1], ALU.subtract), a)
        for r, k in enumerate((0, 0, 1, 1, 0, 2)):
            t_bo6 = load("bo6", bo6[r:r + 1, :], bp[k][r:r + 1, :], a, bz)
        a = A("a_w", lambda e: e.activation(eb2[:], ebst, ACT.Copy), t_eb)
        t_ebs = V("v_w", lambda e: e.tensor_tensor(eb2[NX:128, :], ebst[NX:128, :], f32(eb2[NX:128, :]), ALU.subtract), a)

        for t in range(DT):
            xin.setdefault(1, []).append(load(f"x1_{t}", X[1][:, t, :], xv[1, t], t_ebs, t_bo6, t_tgm, t_keep, t_wos, t_wrs, t_wqk))
        for slot, late, n, fn, args in todo[len(first):]:
            fn(*args)

        Q.wait("sync", *[st_["out", NB - 1, t] for t in range(DT)])

        block = st.enter_context(nc.Block())

        @block.sync
        def _(e):
            Q.play("sync", e)

        @block.scalar
        def _(e):
            Q.play("scalar", e)

        @block.vector
        def _(e):
            Q.play("vector", e)

        @block.gpsimd
        def _(e):
            Q.play("gpsimd", e)

        @block.tensor
        def _(e):
            Q.play("tensor", e)


def kernel(x, ctx_4096, mask_Bx1x4096_ff1, g_xattn, g_ffn, L0_xattn_Wq, L0_xattn_bq, L0_xattn_Wk, L0_xattn_bk,
           L0_xattn_Wv, L0_xattn_bv, L0_xattn_Wo, L0_xattn_bo, L0_ffn_router_weight, L0_ffn_router_bias,
           L0_ffn_expert_bias):
    import numpy as np
    import concourse.bacc as bacc
    from concourse.bass_utils import run_bass_kernel_spmd

    def c(a):
        return np.ascontiguousarray(np.asarray(a))

    arrays = {
        "x": c(x), "ctx": c(ctx_4096), "mask": c(mask_Bx1x4096_ff1), "g_x": c(g_xattn), "g_f": c(g_ffn),
        "wqT": c(np.asarray(L0_xattn_Wq).T), "wkT": c(np.asarray(L0_xattn_Wk).T), "wvT": c(np.asarray(L0_xattn_Wv).T),
        "woT": c(np.asarray(L0_xattn_Wo).T),
        "bq": c(np.asarray(L0_xattn_bq).reshape(2, 128).T), "bk": c(np.asarray(L0_xattn_bk).reshape(2, 128).T),
        "bv": c(L0_xattn_bv), "bo": c(L0_xattn_bo),
        "wrT": c(np.asarray(L0_ffn_router_weight).T), "rb": c(L0_ffn_router_bias), "eb": c(L0_ffn_expert_bias),
    }
    nc = bacc.Bacc("TRN2", target_bir_lowering=False, num_devices=1, dynamic_dma_scratch_size=1024)
    args = [nc.dram_tensor("in_" + n, a.shape, mybir.dt.from_np(a.dtype), kind="ExternalInput").ap()
            for n, a in arrays.items()]
    args.append(nc.dram_tensor("out_y", (NB, D, S), F32, kind="ExternalOutput").ap())
    gated_block_kernel(nc, *args)
    r = run_bass_kernel_spmd(nc, [{"in_" + n: a for n, a in arrays.items()}], core_ids=[0])
    return r.results[0]["out_y"]
```

```python
from contextlib import ExitStack

import concourse.bass as bass
from concourse import mybir

F32 = mybir.dt.float32
F32R = mybir.dt.float32r
BF16 = mybir.dt.bfloat16
F16 = mybir.dt.float16
ALU = mybir.AluOpType
ACT = mybir.ActivationFunctionType
AX = mybir.AxisListType

NB, D, S = 8, 512, 2048
DT = D // 128
E = 256
H, DH = 8, 32
W = 128
U = 256
NU = S // U
SB = S // 128
NX = 64
EPS = 1e-5
SHIFT = 9.0
BIG = 1e9
QSCALE = 1.0 / float(DH) ** 0.5


def bf16_parts(v):
    import numpy as np
    parts, rest = [], np.float32(v)
    for _ in range(3):
        bits = np.array([rest], np.float32).view(np.uint32)
        bits = (bits + 0x7FFF + ((bits >> 16) & 1)) & np.uint32(0xFFFF0000)
        p = bits.view(np.float32)[0]
        parts.append(float(p))
        rest = np.float32(rest - p)
    return parts


SLOTS = dict(
    rows=-11.75, z32=-23, z_hi=-20.25, z_lo=-18.75, q=-16, q_gap=0.375, q_hi=-13, q_lo=-12, k=-13, k_gap=1,
    k32=-11, k_hi=-10, k_lo=-9.25, kz_hi=-9.5, kz_lo=-7.75, kz_gap=6.875, mk=-31, mkb=-19.5,
    c_hi=-15.25, c_lo=-12.75, v=-9.25, v_gap=-0.25, v32=-7.75, v1=-7.5, vr=-4.25, v2=-2.5, v3=-2,
    s0=0, s1=2, s2=0.25, s3=0, S=-0.75, top=0.75, sub=1.25, exp=2.25, PT=5, pt_hi=5.5, pt_lo=6.75, PV=9.25,
    rc=9.75, on=10,
    pair=7.75, gelu=38.25, g2=39, OT=42.75, ot_hi=42.75, ot_lo=43.25, WO=45.5, WO_gap=2.5, x1=47.25, bn2=53.5,
    norm2=30, R0=31.25, R_gap=17.75, h_gap=2, h=-1, hT=2.25, ht_hi=3, ht_lo=4, R=6.5, L=5, LT=5, c_top=6.5,
    c_exp=6.5, c_w=9.5, wT=10.75, wt_hi=12.25, wt_lo=12.25, xa=12.25, m_gap=0.875, mix=14.75, x2=16, rl=20,
    rl_gap=0,
    x_1=0.5, x_gap=3.75, bn1=73, bn1_gap=2, norm1=104.5,
)


SIDE = dict(cx_lo="gpsimd", z_lo="gpsimd", k_lo="gpsimd", vr="gpsimd", v3="gpsimd")


class Queues:

    def __init__(self, make):
        self.make, self.sems, self.count = make, {}, {}
        self.list = {e: [] for e in ("sync", "scalar", "vector", "gpsimd", "tensor")}
        self.seen = {e: {} for e in self.list}

    def op(self, eng, sem, fn, *waits, inc=1):
        if sem not in self.sems:
            self.sems[sem], self.count[sem] = self.make(sem), 0
        for name, n in waits:
            if self.seen[eng].get(name, 0) < n:
                self.seen[eng][name] = n
                self.list[eng].append(("wait", name, n))
        self.count[sem] += inc
        self.list[eng].append(("do", fn, sem, inc))
        return sem, self.count[sem]

    def wait(self, eng, *waits):
        for name, n in waits:
            if self.seen[eng].get(name, 0) < n:
                self.seen[eng][name] = n
                self.list[eng].append(("wait", name, n))

    def play(self, eng, e):
        for it in self.list[eng]:
            if it[0] == "wait":
                e.wait_ge(self.sems[it[1]], it[2])
            else:
                it[1](e).then_inc(self.sems[it[2]], it[3])


def gated_block_kernel(nc, x, ctx, mask, g_x, g_f, wqT, wkT, wvT, woT, bq, bk, bv, bo, wrT, rb, eb, out):
    with ExitStack() as st:
        def sb(name, shape, dt=F32):
            return st.enter_context(nc.sbuf_tensor(name, shape, dt))

        def pb(name):
            return st.enter_context(nc.psum_tensor(name, [128, 512], F32))

        Q = Queues(lambda n: st.enter_context(nc.semaphore("s_" + n)))
        op = Q.op

        X = [sb(f"X{i}", [128, DT, S]) for i in range(2)]
        wqk_hi = sb("wqk_hi", [128, DT, 2 * E], F32R)
        wqk_lo = sb("wqk_lo", [128, DT, 2 * E], F32R)
        wv_hi = sb("wv_hi", [128, DT, E], F32R)
        wv_lo = sb("wv_lo", [128, DT, E], F32R)
        wo_hi = sb("wo_hi", [128, 2, D], F32R)
        wo_lo = sb("wo_lo", [128, 2, D], F32R)
        wr2 = sb("wr2", [128, SB, 2 * NX], F32R)
        eb2 = sb("eb2", [128, S], F32R)
        NK = 3
        kz_hi = [sb(f"kz_hi{i}", [128, 2, 4, W], F32R) for i in range(NK)]
        kz_lo = [sb(f"kz_lo{i}", [128, 2, 4, W], F32R) for i in range(NK)]
        z32 = sb("z32", [128, DT, U])
        z_hi = sb("z_hi", [128, DT, U], F32R)
        z_lo = sb("z_lo", [128, DT, U], F32R)
        NC = 2
        cx = [sb(f"cx{i}", [128, DT, W]) for i in range(NC)]
        cx_hi = sb("cx_hi", [128, DT, W], F32R)
        cx_lo = sb("cx_lo", [128, DT, W], F32R)
        q_hi = [sb(f"q_hi{i}", [128, 2, U], F32R) for i in range(2)]
        q_lo = [sb(f"q_lo{i}", [128, 2, U], F32R) for i in range(2)]
        k32 = sb("k32", [128, 2, U])
        k_hi = sb("k_hi", [128, 2, U], F32R)
        k_lo = sb("k_lo", [128, 2, U], F32R)
        NP = 2
        P32 = [sb(f"P32_{i}", [128, 4, W]) for i in range(NP)]
        pt_hi = [sb(f"pt_hi{i}", [128, 4, W], F16) for i in range(2)]
        pt_lo = [sb(f"pt_lo{i}", [128, 4, W], F16) for i in range(2)]
        NV = 3
        NRW = 4
        v32 = sb("v32", [128, H, DH])
        vp = [[sb(f"v{k}_{i}", [128, H, DH + 1], BF16) for k in range(3)] for i in range(NV)]
        oo = [sb(f"oo{i}", [128, 2, 2, E]) for i in range(2)]
        o32 = [oo[i // 2][:, i % 2, :, :] for i in range(4)]
        ot_hi = sb("ot_hi", [128, 2, U], F32R)
        ot_lo = sb("ot_lo", [128, 2, U], F32R)
        hc = [sb(f"hc{i}", [128, 2, U]) for i in range(2)]
        ht_hi = [sb(f"ht_hi{i}", [128, 2, U], F32R) for i in range(2)]
        ht_lo = [sb(f"ht_lo{i}", [128, 2, U], F32R) for i in range(2)]
        rows = [sb(f"rows{i}", [128, U], BF16) for i in range(NRW)]
        mk = [sb(f"mk{i}", [128, U]) for i in range(2)]
        ident = sb("ident", [128, 128])
        id2 = sb("id2", [128, NX])
        ones3 = sb("ones3", [128, 128], BF16)
        bo6 = sb("bo6", [128, D], BF16)
        cst = sb("cst", [128, 24])
        bvb = sb("bvb", [128, E])
        rbb = sb("rbb", [128, NX])
        tgm = sb("tgm", [128, 128])
        bnst = sb("bnst", [128, DT, 4, 6])
        mv = sb("mv", [128, DT, 2])
        bn2 = sb("bn2", [128, DT, 4, 6])
        mv2 = sb("mv2", [128, DT, 2])
        ln1 = [sb(f"ln1_{i}", [128, 3, DT]) for i in range(2)]
        ln2 = sb("ln2", [128, 3, DT])
        mx = sb("mx", [128, 4, 4])
        rc = sb("rc", [128, 2, H])
        L = sb("L", [128, U])
        lg = sb("lg", [128, 2, NX])
        lr = sb("lr", [128, 2, NX])
        ex = sb("ex", [128, 2, NX])
        w2 = sb("w2", [128, 2, 2 * NX])
        t8 = sb("t8", [128, 2, 8])
        sc = sb("sc", [128, 2, 8])
        wt_hi = sb("wt_hi", [128, 2, 128], F32R)
        wt_lo = sb("wt_lo", [128, 2, 128], F32R)
        half = sb("half", [128, DT])

        NR = 6
        ring = [pb(f"ring{i}") for i in range(NR)]
        idle = [(i, ()) for i in range(NR)]
        PO = pb("PO")
        PR = pb("PR")

        def take():
            assert idle, "no bank: its readers are queued too late"
            i, w = idle.pop(0)
            return i, ring[i], w

        def give(i, *readers):
            idle.append((i, readers))

        def mm(*parts):
            def fn(e):
                for o, a, b, s0, s1 in parts:
                    last = e.matmul(o, a, b, start=s0, stop=s1)
                return last
            return fn

        def tr(*parts):
            def fn(e):
                for o, a, i in parts:
                    last = e.transpose(o, a, i)
                return last
            return fn

        def f32(ap):
            return ap.bitcast(F32)

        BQ, BK, TG, TF, SH, M05 = 0, 2, 4, 5, 6, 7

        stage = X[1]
        wst = stage[:, 0, :].rearrange("p (k n) -> p k n", k=DT)

        def load(sem, dst, src, *waits):
            return op("sync", sem, lambda e: e.dma_start(dst, src), *waits, inc=16)

        xv = x.rearrange("b (t p) s -> b t p s", p=128)
        ov = out.rearrange("b (t p) s -> b t p s", p=128)
        cv = ctx.rearrange("b (t p) s -> b p t s", p=128)
        mflat = mask.rearrange("b o s -> (b o) s")

        def G(sem, fn, *w):
            return op("gpsimd", sem, fn, *w)

        def V(sem, fn, *w):
            return op("vector", sem, fn, *w)

        def A(sem, fn, *w):
            return op("scalar", sem, fn, *w)

        def Z(sem, fn, *w):
            return op(SIDE[sem], sem, fn, *w)

        def T(sem, fn, *w):
            return op("tensor", sem, fn, *w)

        st_ = {}
        TU = NB * NU

        def load_ctx(p):
            b, w = divmod(p, S // W)
            i = p % NC
            free = (st_["cx_lo", p - NC],) if p >= NC else ()
            st_["cx", p] = load(f"cx{i}", cx[i][:], cv[b][:, :, w * W:(w + 1) * W], *free)

        def load_mask(u):
            b, c = divmod(u, NU)
            i = u % 2
            free = (st_["k32", u - 2],) if u >= 2 else ()
            st_["mkl", u] = load(f"mk{i}", mk[i][:], mflat[b:b + 1, c * U:(c + 1) * U].to_broadcast([128, U]), *free)

        def mask_bits(u):
            i = u % 2
            st_["mk", u] = G("mk01", lambda e: e.tensor_scalar(mk[i][:], mk[i][:], 0.0, None, ALU.is_gt), st_["mkl", u])

        load("w_x", cst[:, TG:TG + 1], g_x[None, :].to_broadcast([128, 1]))
        load("w_x", cst[:, TF:TF + 1], g_f[None, :].to_broadcast([128, 1]))
        load("w_x", cst[:, BQ:BQ + 2], bq)
        t_small = load("w_x", cst[:, BK:BK + 2], bk)
        x_in = [[load(f"x0_{t}", X[0][:, t, :], xv[0, t]) for t in range(DT)]]
        for u in range(2):
            load_mask(u)
        load("w_qk", wst[:, :, 0:E], wqT.rearrange("(k p) n -> p k n", p=128))
        t_qk = load("w_qk", wst[:, :, E:2 * E], wkT.rearrange("(k p) n -> p k n", p=128))
        wvst = stage[:, 3, 1024:2048].rearrange("p (k n) -> p k n", k=DT)
        t_wv0 = load("w_v", wvst, wvT.rearrange("(k p) n -> p k n", p=128))
        t_bv = load("w_bv", bvb[:], bv[None, :].to_broadcast([128, E]))
        mT = stage[:, 1, 0:128]
        t_mT = load("w_mT", mT, mflat.rearrange("b (w i) -> (b w) i", i=128))
        mneg = stage[:, 1, 640:768]
        for p in range(NC):
            load_ctx(p)
        wost = stage[:, 1, 1024:2048].rearrange("p (k n) -> p k n", k=2)
        t_wo = load("w_o", wost, woT.rearrange("(k p) n -> p k n", p=128))
        bost = hc[0][0:6].rearrange("p a n -> p (a n)")
        t_bo = load("w_bo", bost, bo[None, :].to_broadcast([6, D]))
        t_rb = load("w_rb", rbb[:], rb[None, :].to_broadcast([128, NX]))
        wrst = stage[:, 3, 0:1024].rearrange("p (k n) -> p k n", k=SB)
        t_wr = load("w_r", wrst, wrT.rearrange("(k p) n -> p k n", p=128))
        ebst = stage[:, 2, :]
        load("w_eb", ebst[0:NX, :], eb)
        t_eb = load("w_eb", ebst[NX:128, :], eb)

        a = G("g_set", lambda e: e.memset(ident[:], 0.0))
        t_id = G("g_set", lambda e: e.affine_select(out=ident[:], in_=ident[:], compare_op=ALU.not_equal, fill=1.0,
                                                   base=0, pattern=[[-1, 128]], channel_multiplier=1), a)
        b = G("g_set", lambda e: e.memset(id2[:], 0.0))
        b = G("g_set", lambda e: e.affine_select(out=id2[:], in_=id2[:], compare_op=ALU.not_equal, fill=1.0,
                                                 base=0, pattern=[[-1, NX]], channel_multiplier=1), b)
        t_id2 = G("g_set", lambda e: e.affine_select(out=id2[:], in_=id2[:], compare_op=ALU.not_equal, fill=1.0,
                                                     base=-NX, pattern=[[-1, NX]], channel_multiplier=1), b)
        G("g_set", lambda e: e.memset(half[:], -0.5))
        t_cst = G("g_set", lambda e: e.memset(cst[:, SH:SH + 1], SHIFT))
        t_vone = [G("g_set", lambda e, i=i, k=k: e.memset(vp[i][k][:, :, DH:DH + 1], 1.0 if k == 0 else 0.0))
                  for i in range(NV) for k in range(3)][-1]
        a = V("v_set", lambda e: e.memset(ones3[:], 1.0))
        bz = V("v_set", lambda e: e.memset(bo6[:], 0.0))
        for i in range(NRW):
            t_rz = V("v_set", lambda e, i=i: e.memset(rows[i][:], 0.0))
        a = G("g_set", lambda e: e.affine_select(out=ones3[:], in_=ones3[:], compare_op=ALU.is_ge, fill=0.0,
                                                 base=-6, pattern=[[0, 128]], channel_multiplier=1), a)
        t_ones3 = G("g_set", lambda e: e.affine_select(out=ones3[:], in_=ones3[:], compare_op=ALU.is_ge, fill=0.0,
                                                       base=8, pattern=[[0, 128]], channel_multiplier=-1), a)

        for i in range(NK):
            G("g_kz", lambda e, i=i: e.memset(f32(kz_hi[i][:]), 0.0))
            t_kz0 = G("g_kz", lambda e, i=i: e.memset(f32(kz_lo[i][:]), 0.0))

        t_tg = A("a_set", lambda e: e.activation(cst[:, TG:TG + 2], cst[:, TG:TG + 2], ACT.Tanh), t_small)
        t_bq = V("v_set", lambda e: e.tensor_scalar(cst[:, BQ:BQ + 2], cst[:, BQ:BQ + 2], QSCALE, None, ALU.mult), t_small)

        def stats1(b, t, r, xin):
            return V("bn1", lambda e: e.bn_stats(bnst[:, t, r, :], X[b % 2][:, t, r * 512:(r + 1) * 512]), xin)

        def norm1(b, last, free):
            l = ln1[b % 2]
            for t in range(DT):
                v = V("bn1a", lambda e, t=t: e.bn_aggr(mv[:, t, :], bnst[:, t, :, :].rearrange("p a c -> p (a c)")), last, free)
            V("bn1b", lambda e: e.tensor_scalar(l[:, 0, :], mv[:, :, 0], -1.0, None, ALU.mult), v)
            v = V("bn1b", lambda e: e.tensor_scalar(l[:, 1, :], mv[:, :, 1], EPS, None, ALU.add))
            return G("rstd1", lambda e: e.tensor_tensor(l[:, 2, :], l[:, 1, :], half[:], ALU.pow), v)

        for t in range(DT):
            for r in range(4):
                last = stats1(0, t, r, x_in[0][t])
        n1 = {0: norm1(0, last, t_cst)}

        V("v_w", lambda e: e.tensor_scalar(wst[:, :, 0:E], wst[:, :, 0:E], QSCALE, None, ALU.mult), t_qk)
        a = V("v_w", lambda e: e.tensor_copy(wqk_hi[:, :, E:2 * E], wst[:, :, E:2 * E]))
        a = V("v_w", lambda e: e.tensor_copy(wqk_hi[:, :, 0:E], wst[:, :, 0:E]), a)
        t_wqk = V("v_w", lambda e: e.tensor_tensor(wqk_lo[:], wst, f32(wqk_hi[:]), ALU.subtract), a)
        a = A("a_w", lambda e: e.activation(wv_hi[:], wvst, ACT.Copy), t_wv0)
        t_wv = V("v_w", lambda e: e.tensor_tensor(wv_lo[:], wvst, f32(wv_hi[:]), ALU.subtract), a)
        tgr = stage[:, 1, 128:256]
        keep = stage[:, 1, 256:640].bitcast(BF16).rearrange("p (k i) -> p k i", k=6)
        rows_d = nc.dram_tensor("rows_d", (9, 128, 128), BF16, kind="Internal").ap()
        V("v_m", lambda e: e.tensor_scalar(tgr, mT, cst[:, TG:TG + 1], None, ALU.mult), t_mT, t_tg)
        a = V("v_m", lambda e: e.tensor_scalar(mneg, mT, 0.0, 1.0, ALU.is_gt, ALU.subtract))
        for k, part in enumerate(bf16_parts(BIG)):
            V("v_m", lambda e, k=k, part=part: e.tensor_scalar(keep[:, 3 + k, :], mneg, part, None, ALU.mult), a)
        a = V("v_m", lambda e: e.tensor_copy(keep[:, 0, :], tgr), a)
        a = V("v_m", lambda e: e.tensor_tensor(tgr, tgr, keep[:, 0, :], ALU.subtract), a)
        a = V("v_m", lambda e: e.tensor_copy(keep[:, 1, :], tgr), a)
        a = V("v_m", lambda e: e.tensor_tensor(keep[:, 2, :], tgr, keep[:, 1, :], ALU.subtract), a)
        for k0, src in ((0, keep[:, 0:2, :]), (2, keep[:, 0:3, :]), (5, keep[:, 0:1, :]), (6, keep[:, 3:6, :])):
            n = src.shape[1]
            t_keep = load("rows_d", rows_d[k0:k0 + n].rearrange("k p i -> p k i"), src, a)
        i, bank, w = take()
        a = T("setT", lambda e, bank=bank: e.transpose(bank[:, 0:128], mT, ident[:]), t_mT, t_id, *w)
        t_tgm = V("v_m", lambda e, bank=bank: e.tensor_scalar(tgm[:], bank[:, 0:128], cst[:, TG:TG + 1], None, ALU.mult), a, t_tg)
        give(i, t_tgm)

        def load_rows(u):
            free = (st_["WO", u - NRW, 1],) if u >= NRW else (t_keep, t_rz)
            st_["rows", u] = load(f"rows{u % NRW}", rows[u % NRW][0:9, :],
                                  rows_d[:, 2 * u:2 * u + 2, :].rearrange("k w i -> k (w i)"), *free)


        def z_full(u):
            b, c = divmod(u, NU)
            l = ln1[b % 2]
            free = (st_["z_lo", u - 1],) if u else ()
            for t in range(DT):
                z = G("z32", lambda e, t=t: e.tensor_scalar(z32[:, t, :], X[b % 2][:, t, c * U:(c + 1) * U],
                                                            l[:, 0, t:t + 1], l[:, 2, t:t + 1], ALU.add, ALU.mult),
                      n1[b], *free)
            st_["z32", u] = z

        def z_high(u):
            free = (st_["qk", u - 1, 1, 1],) if u else ()
            st_["z_hi", u] = A("z_hi", lambda e: e.activation(z_hi[:], z32[:], ACT.Copy), st_["z32", u], *free)

        def z_low(u):
            free = (st_["qk", u - 1, 1, 1],) if u else ()
            st_["z_lo", u] = Z("z_lo", lambda e: e.tensor_tensor(z_lo[:], z32[:], f32(z_hi[:]), ALU.subtract),
                               st_["z_hi", u], *free)

        def project(u, kind, m):
            if m == 0:
                st_["qkb", u, kind] = take()
            i, bank, w = st_["qkb", u, kind]
            parts = []
            n = 0
            for t in range(DT):
                cols = slice(kind * E + m * 128, kind * E + (m + 1) * 128)
                for a_, z_ in ((wqk_hi, z_hi), (wqk_lo, z_hi), (wqk_hi, z_lo)):
                    parts.append((bank[:, m * U:(m + 1) * U], a_[:, t, cols], z_[:, t, :], n == 0, n == 3 * DT - 1))
                    n += 1
            st_["qk", u, kind, m] = T("qk", mm(*parts), st_["z_hi", u], st_["z_lo", u], t_wqk, *w)

        def q_high(u):
            i, bank, _ = st_["qkb", u, 0]
            free = (st_["S", 4 * (u - 2) + 3],) if u >= 2 else ()
            for m in range(2):
                st_["q_hi", u] = A("q_hi", lambda e, m=m: e.activation(
                    q_hi[u % 2][:, m, :], bank[:, m * U:(m + 1) * U], ACT.Identity, bias=cst[:, BQ + m:BQ + m + 1]),
                    st_["qk", u, 0, 1], t_bq, *free)

        def q_low(u):
            i, bank, _ = st_["qkb", u, 0]
            free = (st_["S", 4 * (u - 2) + 3],) if u >= 2 else ()
            for m in range(2):
                l = V("q_lo", lambda e, m=m: e.scalar_tensor_tensor(
                    out=q_lo[u % 2][:, m, :], in0=bank[:, m * U:(m + 1) * U], scalar=cst[:, BQ + m:BQ + m + 1],
                    in1=f32(q_hi[u % 2][:, m, :]), op0=ALU.add, op1=ALU.subtract), st_["q_hi", u], t_bq, *free)
            give(i, l)
            st_["q", u] = (st_["q_hi", u], l)

        def k_full(u):
            i, bank, _ = st_["qkb", u, 1]
            free = (st_["k_lo", u - 1],) if u else ()
            for m in range(2):
                v = V("k32", lambda e, m=m: e.scalar_tensor_tensor(
                    out=k32[:, m, :], in0=bank[:, m * U:(m + 1) * U], scalar=cst[:, BK + m:BK + m + 1], in1=mk[u % 2][:],
                    op0=ALU.add, op1=ALU.mult), st_["qk", u, 1, 1], st_["mk", u], *free)
            give(i, v)
            st_["k32", u] = v

        def k_spread(p, n, src, dst):
            u, w = divmod(p, 2)
            free = (st_["S", 2 * (p - NK) + 1],) if p >= NK else (t_kz0,)
            for g in range(4):
                st_["kz", p, n] = load(f"kz{p % NK}_{n}", f32(dst[32 * g:32 * g + 32, :, g, :]),
                                       f32(src[32 * g:32 * g + 32, :, w * W:(w + 1) * W]),
                                       st_[("k_hi", "k_lo")[n], u], *free)

        def spread_high(p):
            k_spread(p, 0, k_hi, kz_hi[p % NK])

        def spread_low(p):
            k_spread(p, 1, k_lo, kz_lo[p % NK])

        def k_high(u):
            free = (st_["kz", 2 * u - 2, 0], st_["kz", 2 * u - 1, 0]) if u else ()
            st_["k_hi", u] = A("k_hi", lambda e: e.activation(k_hi[:], k32[:], ACT.Copy), st_["k32", u], *free)

        def k_low(u):
            free = (st_["kz", 2 * u - 2, 1], st_["kz", 2 * u - 1, 1]) if u else ()
            st_["k_lo", u] = Z("k_lo", lambda e: e.tensor_tensor(k_lo[:], k32[:], f32(k_hi[:]), ALU.subtract),
                               st_["k_hi", u], st_["k32", u], *free)

        def c_high(p):
            free = (st_["v", p - 1],) if p else ()
            st_["cx_hi", p] = A("cx_hi", lambda e: e.activation(cx_hi[:], cx[p % NC][:], ACT.Copy), st_["cx", p], *free)

        def c_low(p):
            free = (st_["v", p - 1],) if p else ()
            st_["cx_lo", p] = Z("cx_lo", lambda e: e.tensor_tensor(cx_lo[:], cx[p % NC][:], f32(cx_hi[:]), ALU.subtract),
                                st_["cx_hi", p], st_["cx", p], *free)
            if p + NC < 2 * TU:
                load_ctx(p + NC)

        def v_mm(p):
            i, bank, w = take()
            parts = []
            for k in range(DT):
                for c_, w_ in ((cx_hi, wv_hi), (cx_hi, wv_lo), (cx_lo, wv_hi)):
                    n = len(parts)
                    parts.append((bank[:, 0:E], c_[:, k, :], w_[:, k, :], n == 0, n == 3 * DT - 1))
            st_["v", p] = T("v", mm(*parts), st_["cx_hi", p], st_["cx_lo", p], t_wv, *w)
            st_["vb", p] = i, bank

        def v_full(p):
            i, bank = st_["vb", p]
            prev = (st_["v3", p - 1],) if p else ()
            a = V("v32", lambda e: e.tensor_tensor(v32[:], bank[:, 0:E].rearrange("p (h d) -> p h d", h=H),
                                                   bvb[:].rearrange("p (h d) -> p h d", h=H), ALU.add),
                  st_["v", p], t_bv, *prev)
            give(i, a)
            st_["v32", p] = a

        def v_1(p):
            free = (st_["PV", 2 * (p - NV) + 1],) if p >= NV else (t_vone,)
            st_["v1", p] = A("v1", lambda e: e.activation(vp[p % NV][0][:, :, 0:DH], v32[:], ACT.Copy), st_["v32", p], *free)

        def v_r(p):
            st_["vr", p] = Z("vr", lambda e: e.tensor_tensor(v32[:], v32[:], vp[p % NV][0][:, :, 0:DH], ALU.subtract),
                             st_["v1", p], st_["v32", p])

        def v_2(p):
            st_["v2", p] = A("v2", lambda e: e.activation(vp[p % NV][1][:, :, 0:DH], v32[:], ACT.Copy), st_["vr", p])

        def v_3(p):
            st_["v3", p] = Z("v3", lambda e: e.tensor_tensor(vp[p % NV][2][:, :, 0:DH], v32[:], vp[p % NV][1][:, :, 0:DH],
                                                             ALU.subtract), st_["v2", p], st_["vr", p], st_["v1", p])

        def scores(s):
            u, k = divmod(s, 4)
            w, m = divmod(k, 2)
            i, bank, fr = take()
            cols = slice(w * W, (w + 1) * W)
            p = 2 * u + w
            kh, kl = kz_hi[p % NK][:, m, :, :], kz_lo[p % NK][:, m, :, :]
            qh, ql = q_hi[u % 2][:, m, cols], q_lo[u % 2][:, m, cols]
            mrow = rows[u % NRW][:, cols].unsqueeze(1).to_broadcast([128, 4, W])
            o = bank[:].rearrange("p (h j) -> p h j", h=4)
            st_["S", s] = T("S", mm((o, ones3[:], mrow, True, False), (o, qh, kh, False, False),
                                    (o, ql, kh, False, False), (o, qh, kl, False, True)),
                            *st_["q", u], st_["kz", p, 0], st_["kz", p, 1], st_["rows", u], t_ones3, *fr)
            st_["Sb", s] = i, o

        def top(s):
            i, o = st_["Sb", s]
            m = mx[:, s % 4, :]
            st_["mx", s] = V("mx", lambda e: e.tensor_reduce(m, o, AX.X, ALU.max), st_["S", s])

        def center(s):
            i, o = st_["Sb", s]
            m = mx[:, s % 4, :]
            free = (st_["PT", s - NP],) if s >= NP else ()
            v = V("sub", lambda e: e.tensor_tensor(P32[s % NP][:], o, m.unsqueeze(2).to_broadcast([128, 4, W]),
                                                   ALU.subtract), st_["mx", s], *free)
            give(i, v)
            st_["sub", s] = v

        def expo(s):
            P = P32[s % NP]
            st_["exp", s] = A("exp", lambda e: e.activation(P[:], P[:], ACT.Exp, bias=cst[:, SH:SH + 1]), st_["sub", s], t_cst)

        def turn_p(s):
            i, bank, fr = take()
            P = P32[s % NP]
            st_["PT", s] = T("PT", tr(*[(bank[:, h * W:(h + 1) * W], P[:, h, :], ident[:]) for h in range(4)]),
                             st_["exp", s], t_id, *fr)
            st_["PTb", s] = i, bank[:].rearrange("p (h j) -> p h j", h=4)

        def p_high(s):
            i, o = st_["PTb", s]
            free = (st_["PV", s - 2],) if s >= 2 else ()
            st_["pt_hi", s] = A("pt_hi", lambda e: e.activation(pt_hi[s % 2][:], o, ACT.Copy), st_["PT", s], *free)

        def p_low(s):
            i, o = st_["PTb", s]
            free = (st_["PV", s - 2],) if s >= 2 else ()
            l = V("pt_lo", lambda e: e.tensor_tensor(pt_lo[s % 2][:], o, pt_hi[s % 2][:], ALU.subtract),
                  st_["pt_hi", s], *free)
            give(i, l)
            st_["pt_lo", s] = l

        def weigh(s):
            u, k = divmod(s, 4)
            w, m = divmod(k, 2)
            p = 2 * u + w
            vv = vp[p % NV]
            ph, pl = pt_hi[s % 2], pt_lo[s % 2]
            parts = []
            for h in range(4):
                hh = 4 * m + h
                o = PO[:, hh * (DH + 1):(hh + 1) * (DH + 1)]
                for n, (a, k_) in enumerate(((ph, 0), (ph, 1), (ph, 2), (pl, 0), (pl, 1))):
                    parts.append((o, a[:, h, :], vv[k_][:, hh, :], n == 0, n == 4))
            free = (st_["on", p - 1],) if m == 0 and p else ()
            st_["PV", s] = T("PV", mm(*parts), st_["pt_hi", s], st_["pt_lo", s], st_["v1", p], st_["v2", p], st_["v3", p],
                             *free)

        def invert(p):
            o = PO[:, 0:H * (DH + 1)].rearrange("p (h d) -> p h d", h=H)
            st_["rc", p] = V("rc", lambda e: e.reciprocal(rc[:, p % 2, :].unsqueeze(2), o[:, :, DH:DH + 1]),
                             st_["PV", 2 * p + 1])

        def divide(p):
            o = PO[:, 0:H * (DH + 1)].rearrange("p (h d) -> p h d", h=H)
            u, w = divmod(p, 2)
            od = o32[u % 4][:, w, :].rearrange("p (h d) -> p h d", h=H)
            free = (st_["OT", u - 4],) if u >= 4 else ()
            st_["on", p] = V("on", lambda e: e.tensor_tensor(
                od, o[:, :, 0:DH], rc[:, p % 2, :].unsqueeze(2).to_broadcast([128, H, DH]), ALU.mult), st_["rc", p], *free)

        def gelu(u):
            o = oo[u // 2 % 2]
            st_["gelu", u] = st_["gelu", u + 1] = A("gelu", lambda e: e.activation(o[:], o[:], ACT.Gelu),
                                                    st_["on", 2 * u + 3])

        def scale_o(u):
            o = o32[u % 4]
            for w in range(2):
                p = 2 * u + w
                eng, sem = (V, "g2v") if u >= TU - 2 else (G, "g2")
                st_["g2", u] = eng(sem, lambda e, w=w, p=p: e.tensor_scalar(o[:, w, :], o[:, w, :], tgm[:, p:p + 1], None,
                                                                            ALU.mult), st_["gelu", u], t_tgm)

        def turn_o(u):
            i, bank, fr = take()
            st_["OT", u] = T("OT", tr(*[(bank[:, m * U + w * W:m * U + (w + 1) * W],
                                         o32[u % 4][:, w, m * 128:(m + 1) * 128], ident[:])
                                        for m in range(2) for w in range(2)]), st_["g2", u], t_id, *fr)
            st_["OTb", u] = i, bank[:].rearrange("p (m i) -> p m i", m=2)

        def o_high(u):
            i, o = st_["OTb", u]
            free = (st_["WO", u - 1, 1],) if u else ()
            st_["ot_hi", u] = A("ot_hi", lambda e: e.activation(ot_hi[:], o, ACT.Copy), st_["OT", u], *free)

        def o_low(u):
            i, o = st_["OTb", u]
            free = (st_["WO", u - 1, 1],) if u else ()
            l = V("ot_lo", lambda e: e.tensor_tensor(ot_lo[:], o, f32(ot_hi[:]), ALU.subtract), st_["ot_hi", u], *free)
            give(i, l)
            st_["ot_lo", u] = l

        def project_out(u, j):
            b, c = divmod(u, NU)
            i, bank, fr = take()
            parts = []
            for n in range(2):
                t = 2 * j + n
                o = bank[:, n * U:(n + 1) * U]
                cols = slice(t * 128, (t + 1) * 128)
                parts.append((o, bo6[:, cols], rows[u % NRW][:], True, False))
                for m in range(2):
                    for q_, (a, z) in enumerate(((wo_hi, ot_hi), (wo_lo, ot_hi), (wo_hi, ot_lo))):
                        parts.append((o, a[:, m, cols], z[:, m, :], False, m == 1 and q_ == 2))
            st_["WO", u, j] = T("WO", mm(*parts), st_["ot_hi", u], st_["ot_lo", u], st_["rows", u], t_bo6, t_wos, *fr)
            st_["WOb", u, j] = i, bank[:].rearrange("p (n i) -> p n i", n=2)

        def add_x(u, j):
            b, c = divmod(u, NU)
            i, o = st_["WOb", u, j]
            xs = X[b % 2][:, 2 * j:2 * j + 2, c * U:(c + 1) * U]
            v = V("x1", lambda e: e.tensor_tensor(xs, xs, o, ALU.add), st_["WO", u, j])
            give(i, v)
            st_["x1", u, j] = v

        def stats2(b, r):
            for t in range(DT):
                st_["bn2", b, r] = V("bn2", lambda e, t=t: e.bn_stats(bn2[:, t, r, :], X[b % 2][:, t, r * 512:(r + 1) * 512]),
                                  st_["x1", b * NU + 2 * r, 1], st_["x1", b * NU + 2 * r + 1, 1], *((st_["mv2", b - 1],) if b else ()))

        def norm2(b):
            for t in range(DT):
                v = V("mv2", lambda e, t=t: e.bn_aggr(mv2[:, t, :], bn2[:, t, :, :].rearrange("p a c -> p (a c)")),
                      *[st_["bn2", b, r] for r in range(4)])
            st_["mv2", b] = v
            free = (st_["ac", b - 1, 1],) if b else ()
            V("ln2", lambda e: e.tensor_scalar(ln2[:, 0, :], mv2[:, :, 0], -1.0, None, ALU.mult), v, *free)
            v = V("ln2", lambda e: e.tensor_scalar(ln2[:, 1, :], mv2[:, :, 1], EPS, None, ALU.add))
            st_["ln2", b] = G("rstd2", lambda e: e.tensor_tensor(ln2[:, 2, :], ln2[:, 1, :], half[:], ALU.pow), v)

        def r_full(b, j, c):
            n = (b * 2 + j) * NU + c
            free = (st_["hT", n - 2],) if n >= 2 else (t_bos, t_bo6)
            st_["h", n] = ()
            for q_ in range(2):
                t = 2 * j + q_
                eng, sem = (V, "hv") if b == NB - 1 and q_ else (G, "h")
                st_["h", n] += eng(sem, lambda e, q_=q_, t=t: e.tensor_scalar(
                    hc[n % 2][:, q_, :], X[b % 2][:, t, c * U:(c + 1) * U], ln2[:, 0, t:t + 1], ln2[:, 2, t:t + 1],
                    ALU.add, ALU.mult), st_["ln2", b], *free),

        def r_turn(b, j, c):
            n = (b * 2 + j) * NU + c
            i, bank, fr = take()
            st_["hT", n] = T("hT", tr(*[(bank[:, a * U + q_ * 128:a * U + (q_ + 1) * 128],
                                         hc[n % 2][:, q_, a * 128:(a + 1) * 128], ident[:])
                                        for a in range(2) for q_ in range(2)]), *st_["h", n], t_id, *fr)
            st_["hTb", n] = i, bank[:].rearrange("p (a i) -> p a i", a=2)

        def r_high(b, j, c):
            n = (b * 2 + j) * NU + c
            i, o = st_["hTb", n]
            free = (st_["R", n - 2],) if n >= 2 else ()
            st_["ht_hi", n] = A("ht_hi", lambda e: e.activation(ht_hi[n % 2][:], o, ACT.Copy), st_["hT", n], *free)

        def r_low(b, j, c):
            n = (b * 2 + j) * NU + c
            i, o = st_["hTb", n]
            free = (st_["R", n - 2],) if n >= 2 else ()
            l = V("ht_lo", lambda e: e.tensor_tensor(ht_lo[n % 2][:], o, f32(ht_hi[n % 2][:]), ALU.subtract), st_["ht_hi", n], *free)
            give(i, l)
            st_["ht_lo", n] = l

        def r_mm(b, j, c):
            n = (b * 2 + j) * NU + c
            parts = []
            for a in range(2):
                for q_, z in enumerate((ht_hi[n % 2], ht_lo[n % 2])):
                    parts.append((PR[:, 0:U], wr2[:, 2 * c + a, :], z[:, a, :], c == 0 and a == 0 and q_ == 0,
                                  c == NU - 1 and a == 1 and q_ == 1))
            free = (st_["L", b * 2 + j - 1],) if c == 0 and n else ()
            st_["R", n] = T("R", mm(*parts), st_["ht_hi", n], st_["ht_lo", n], t_wrs, *free)

        def c_logits(b, j):
            n = b * 2 + j
            free = (st_["LT", n - 1],) if n else ()
            st_["L", n] = A("L", lambda e: e.activation(L[:], PR[:, 0:U], ACT.Copy), st_["R", n * NU + NU - 1], *free)

        def c_turn(b, j):
            n = b * 2 + j
            i, bank, fr = take()
            st_["LT", n] = T("LT", mm(*[(bank[:, q_ * NX:(q_ + 1) * NX], L[:, q_ * 128:(q_ + 1) * 128], id2[:], True, True)
                                        for q_ in range(2)]), st_["L", n], t_id2, *fr)
            st_["LTb", n] = i, bank[:, 0:2 * NX].rearrange("p (q x) -> p q x", q=2)

        def c_top(b, j):
            n = b * 2 + j
            i, o = st_["LTb", n]
            free = (st_["w2", n - 1],) if n else ()
            v = V("lg", lambda e: e.tensor_tensor(lg[:], o, rbb[:].unsqueeze(1).to_broadcast([128, 2, NX]), ALU.add),
                  st_["LT", n], t_rb, *free)
            give(i, v)
            for q_ in range(2):
                v1 = V("top", lambda e, q_=q_: e.max(t8[:, q_, :], lg[:, q_, :]), v)
            v2 = V("neg", lambda e: e.tensor_scalar(sc[:, :, 0:1], t8[:, :, 0:1], -1.0, None, ALU.mult), v1, *(
                [st_["xa", (n - 1) // 2, (n - 1) % 2 * 2 + q_] for q_ in range(2)] if n else ()))
            st_["neg", n] = v2
            for q_ in range(2):
                v3 = V("top", lambda e, q_=q_: e.match_replace(lr[:, q_, :], t8[:, q_, :], lg[:, q_, :], -3.0e38), v1)
            st_["sel", n] = V("top", lambda e: e.tensor_tensor(lr[:], lr[:], lg[:], ALU.not_equal), v3)

        def c_exp(b, j):
            n = b * 2 + j
            for q_ in range(2):
                st_["ex", n] = A("ex", lambda e, q_=q_: e.activation(ex[:, q_, :], lg[:, q_, :], ACT.Exp,
                                                                     bias=sc[:, q_, 0:1], accum_out=sc[:, q_, 1:2]),
                                 st_["neg", n], *((st_["w2", n - 1],) if n else ()))

        def c_weights(b, j):
            n = b * 2 + j
            free = (st_["wT", n - 1],) if n else ()
            v3 = V("top", lambda e: e.tensor_tensor(ex[:], ex[:], lr[:], ALU.mult), st_["ex", n], st_["sel", n])
            v4 = V("top", lambda e: e.reciprocal(sc[:, :, 3:4], sc[:, :, 1:2]))
            v3 = V("top", lambda e: e.tensor_reduce(sc[:, :, 2:3], ex[:], AX.X, ALU.add), v3)
            v4 = V("top", lambda e: e.tensor_scalar(sc[:, :, 4:5], sc[:, :, 3:4], cst[:, TF:TF + 1], None, ALU.mult), v4, t_tg)
            for q_ in range(2):
                v5 = V("w2", lambda e, q_=q_: e.tensor_scalar(
                    w2[:, q_, :].rearrange("p (a x) -> p a x", a=2), ex[:, q_, :].unsqueeze(1).to_broadcast([128, 2, NX]),
                    sc[:, q_, 4:5], None, ALU.mult), v3, v4, *free)
            st_["w2", n] = v5
            v6 = V("top", lambda e: e.tensor_tensor(sc[:, :, 5:6], sc[:, :, 2:3], sc[:, :, 4:5], ALU.mult), v3, v4)
            v6 = V("top", lambda e: e.tensor_tensor(sc[:, :, 5:6], sc[:, :, 5:6], ln2[:, 2, 2 * j:2 * j + 2].unsqueeze(2),
                                                    ALU.mult), v6, st_["ln2", b])
            V("top", lambda e: e.tensor_scalar(sc[:, :, 6:7], sc[:, :, 5:6], 1.0, None, ALU.add), v6)
            st_["ac", b, j] = V("top", lambda e: e.tensor_tensor(sc[:, :, 7:8], sc[:, :, 5:6],
                                                                 ln2[:, 0, 2 * j:2 * j + 2].unsqueeze(2), ALU.mult), v6)

        def w_turn(b, j):
            n = b * 2 + j
            i, bank, fr = take()
            st_["wT", n] = T("wT", tr(*[(bank[:, q_ * 128:(q_ + 1) * 128], w2[:, q_, :], ident[:]) for q_ in range(2)]),
                             st_["w2", n], t_id, *fr)
            st_["wTb", n] = i, bank[:, 0:256].rearrange("p (q t) -> p q t", q=2)

        def w_high(b, j):
            n = b * 2 + j
            i, o = st_["wTb", n]
            free = (st_["mix", n - 1],) if n else ()
            st_["wt_hi", n] = A("wt_hi", lambda e: e.activation(wt_hi[:], o, ACT.Copy), st_["wT", n], *free)

        def w_low(b, j):
            n = b * 2 + j
            i, o = st_["wTb", n]
            free = (st_["mix", n - 1],) if n else ()
            l = V("wt_lo", lambda e: e.tensor_tensor(wt_lo[:], o, f32(wt_hi[:]), ALU.subtract), st_["wt_hi", n], *free)
            give(i, l)
            st_["wt_lo", n] = l

        def scale_x(b, t):
            j, q_ = divmod(t, 2)
            xs = X[b % 2][:, t, :]
            eng, sem = (V, "xav") if b == NB - 1 and q_ else (G, "xa")
            st_["xa", b, t] = eng(sem, lambda e: e.tensor_scalar(xs, xs, sc[:, q_, 6:7], sc[:, q_, 7:8], ALU.mult, ALU.add),
                                st_["ac", b, j], *st_["h", (b * 2 + j) * NU + NU - 1])

        def mix(b, t, c):
            n, q_ = b * 2 + t // 2, t % 2
            i, bank, fr = take()
            cols = slice(c * 512, (c + 1) * 512)
            st_["mix", n] = T("mix", mm((bank[:], wt_hi[:, q_, :], eb2[:, cols], True, False),
                                        (bank[:], wt_lo[:, q_, :], eb2[:, cols], False, True)),
                              st_["wt_hi", n], st_["wt_lo", n], t_ebs, *fr)
            st_["mixb", b, t, c] = i, bank, st_["mix", n]

        def add_mix(b, t, c):
            i, bank, tok = st_["mixb", b, t, c]
            xs = X[b % 2][:, t, c * 512:(c + 1) * 512]
            v = V("x2", lambda e: e.tensor_tensor(xs, xs, bank[:], ALU.add), tok, st_["xa", b, t])
            give(i, v)
            st_["out", b, t] = load(f"out{t}", ov[b, t, :, c * 512:(c + 1) * 512], xs, v)
            st_["outs", b, t, c] = st_["out", b, t]

        loose = []

        def load_x(b, t, c):
            assert b > 1 or loose
            free = loose if b < 2 else (st_["outs", b - 2, t, 3],)
            st_["xin", b, t] = load(f"x{b % 2}_{t}", X[b % 2][:, t, c * 512:(c + 1) * 512],
                                    xv[b, t, :, c * 512:(c + 1) * 512], *free)

        def input_stats(b, t, r):
            assert st_["xin", b, t][1] == 16 * 4 * (b // 2 + 1) - (48 if b % 2 == 0 else 0), "a tile's four loads come first"
            st_["s1", b, t, r] = stats1(b, t, r, st_["xin", b, t])

        def input_norm(b):
            n1[b] = norm1(b, [st_["s1", b, t, r] for t in range(DT) for r in range(4)][-1], n1[b - 1])

        plan = []

        def at(slot, fn, *args):
            plan.append((slot, len(plan), fn, args))

        C = SLOTS
        for u in range(TU):
            o = 16 * u
            at(o + C["rows"], load_rows, u)
            at(o + C["z32"], z_full, u)
            at(o + C["z_hi"], z_high, u)
            at(o + C["z_lo"], z_low, u)
            for m in range(2):
                at(o + C["q"] + m * C["q_gap"], project, u, 0, m)
                at(o + C["k"] + m * C["k_gap"], project, u, 1, m)
            at(o + C["q_hi"], q_high, u)
            at(o + C["q_lo"], q_low, u)
            at(o + C["k32"], k_full, u)
            at(o + C["k_hi"], k_high, u)
            at(o + C["k_lo"], k_low, u)
            for w in range(2):
                at(o + C["kz_hi"] + w * C["kz_gap"], spread_high, 2 * u + w)
                at(o + C["kz_lo"] + w * C["kz_gap"], spread_low, 2 * u + w)
            if u >= 2:
                at(o + C["mk"], load_mask, u)
            at(o + C["mkb"], mask_bits, u)
            for w in range(2):
                p = 2 * u + w
                for d, f in (("c_hi", c_high), ("c_lo", c_low), ("v", v_mm), ("v32", v_full), ("v1", v_1), ("vr", v_r),
                             ("v2", v_2), ("v3", v_3)):
                    at(o + (8 + C["v_gap"]) * w + C[d], f, p)
                at(o + 8 * w + 4 + C["rc"] + C[("s1", "s3")[w]], invert, p)
                at(o + 8 * w + 4 + C["on"] + C[("s1", "s3")[w]], divide, p)
            for k in range(4):
                s = 4 * u + k
                for d, f in (("S", scores), ("top", top), ("sub", center), ("exp", expo), ("PT", turn_p), ("pt_hi", p_high),
                             ("pt_lo", p_low), ("PV", weigh)):
                    at(o + 4 * k + C[d] + C[f"s{k}"], f, s)
            if u % 2 == 0:
                at(o + C["gelu"], gelu, u)
            if u % 2:
                o -= C["pair"]
            for d, f in (("g2", scale_o), ("OT", turn_o), ("ot_hi", o_high), ("ot_lo", o_low)):
                at(o + C[d], f, u)
            for j in range(2):
                at(o + C["WO"] + C["WO_gap"] * j, project_out, u, j)
                at(o + C["x1"] + C["WO_gap"] * j, add_x, u, j)
            if u % 2:
                at(o + C["bn2"], stats2, u // NU, (u % NU) // 2)
        for b in range(NB):
            o = 128 * (b + 1)
            at(o + C["norm2"], norm2, b)
            for j in range(2):
                q = o + C["R0"] + C["R_gap"] * j
                for c in range(NU):
                    for d, f in (("h", r_full), ("hT", r_turn), ("ht_hi", r_high), ("ht_lo", r_low), ("R", r_mm)):
                        at(q + C["h_gap"] * c + C[d], f, b, j, c)
                q += 8 * C["h_gap"]
                for d, f in (("L", c_logits), ("LT", c_turn), ("c_top", c_top), ("c_exp", c_exp), ("c_w", c_weights),
                             ("wT", w_turn), ("wt_hi", w_high), ("wt_lo", w_low)):
                    at(q + C[d], f, b, j)
                for q_ in range(2):
                    at(q + C["xa"] + 3 * q_, scale_x, b, 2 * j + q_)
                    for c in range(4 if b + 2 < NB else 0):
                        at(q + C["rl"] + 4 * C["m_gap"] * q_ + C["rl_gap"] * c, load_x, b + 2, 2 * j + q_, c)
                    for c in range(4):
                        at(q + C["mix"] + C["m_gap"] * (4 * q_ + c), mix, b, 2 * j + q_, c)
                        at(q + C["x2"] + C["m_gap"] * (4 * q_ + c), add_mix, b, 2 * j + q_, c)
            if b == 1:
                for t in range(DT):
                    for c in range(4):
                        at(C["x_1"] + C["x_gap"] * (4 * t + c), load_x, b, t, c)
            if b:
                o = 128 * (b - 1)
                for t in range(DT):
                    for r in range(4):
                        at(o + C["bn1"] + C["bn1_gap"] * (4 * t + r), input_stats, b, t, r)
                at(o + C["norm1"], input_norm, b)

        todo = sorted(plan, key=lambda x: x[:2])
        first = [x for x in todo if x[0] < -6]
        for slot, n, fn, args in first:
            fn(*args)

        a = A("a_w", lambda e: e.activation(wo_hi[:], wost, ACT.Copy), t_wo)
        t_wos = V("v_w", lambda e: e.tensor_tensor(wo_lo[:], wost, f32(wo_hi[:]), ALU.subtract), a)
        a = A("a_w", lambda e: e.activation(wr2[:, :, 0:NX], wrst, ACT.Copy), t_wr)
        t_wrs = V("v_w", lambda e: e.tensor_tensor(wr2[:, :, NX:2 * NX], wrst, f32(wr2[:, :, 0:NX]), ALU.subtract), a)
        bp = [hc[1][0:6, 0, :].bitcast(BF16), hc[1][0:6, 1, :].bitcast(BF16), stage[0:6, 1, 768:1024].bitcast(BF16)]
        a = V("v_w", lambda e: e.tensor_copy(bp[0], bost), t_bo)
        a = V("v_w", lambda e: e.tensor_tensor(bost, bost, bp[0], ALU.subtract), a)
        a = V("v_w", lambda e: e.tensor_copy(bp[1], bost), a)
        t_bos = a = V("v_w", lambda e: e.tensor_tensor(bp[2], bost, bp[1], ALU.subtract), a)
        for r, k in enumerate((0, 0, 1, 1, 0, 2)):
            t_bo6 = load("bo6", bo6[r:r + 1, :], bp[k][r:r + 1, :], a, bz)
        a = A("a_w", lambda e: e.activation(eb2[:], ebst, ACT.Copy), t_eb)
        t_ebs = V("v_w", lambda e: e.tensor_tensor(eb2[NX:128, :], ebst[NX:128, :], f32(eb2[NX:128, :]), ALU.subtract), a)

        loose.extend([t_ebs, t_bo6, t_tgm, t_keep, t_wos, t_wrs, t_wqk, t_wv])
        for slot, n, fn, args in todo[len(first):]:
            fn(*args)

        Q.wait("sync", *[st_["out", NB - 1, t] for t in range(DT)])

        block = st.enter_context(nc.Block())

        @block.sync
        def _(e):
            Q.play("sync", e)

        @block.scalar
        def _(e):
            Q.play("scalar", e)

        @block.vector
        def _(e):
            Q.play("vector", e)

        @block.gpsimd
        def _(e):
            Q.play("gpsimd", e)

        @block.tensor
        def _(e):
            Q.play("tensor", e)


def kernel(x, ctx_4096, mask_Bx1x4096_ff1, g_xattn, g_ffn, L0_xattn_Wq, L0_xattn_bq, L0_xattn_Wk, L0_xattn_bk,
           L0_xattn_Wv, L0_xattn_bv, L0_xattn_Wo, L0_xattn_bo, L0_ffn_router_weight, L0_ffn_router_bias,
           L0_ffn_expert_bias):
    import numpy as np
    import concourse.bacc as bacc
    from concourse.bass_utils import run_bass_kernel_spmd

    def c(a):
        return np.ascontiguousarray(np.asarray(a))

    arrays = {
        "x": c(x), "ctx": c(ctx_4096), "mask": c(mask_Bx1x4096_ff1), "g_x": c(g_xattn), "g_f": c(g_ffn),
        "wqT": c(np.asarray(L0_xattn_Wq).T), "wkT": c(np.asarray(L0_xattn_Wk).T), "wvT": c(np.asarray(L0_xattn_Wv).T),
        "woT": c(np.asarray(L0_xattn_Wo).T),
        "bq": c(np.asarray(L0_xattn_bq).reshape(2, 128).T), "bk": c(np.asarray(L0_xattn_bk).reshape(2, 128).T),
        "bv": c(L0_xattn_bv), "bo": c(L0_xattn_bo),
        "wrT": c(np.asarray(L0_ffn_router_weight).T), "rb": c(L0_ffn_router_bias), "eb": c(L0_ffn_expert_bias),
    }
    nc = bacc.Bacc("TRN2", target_bir_lowering=False, num_devices=1, dynamic_dma_scratch_size=1024)
    args = [nc.dram_tensor("in_" + n, a.shape, mybir.dt.from_np(a.dtype), kind="ExternalInput").ap()
            for n, a in arrays.items()]
    args.append(nc.dram_tensor("out_y", (NB, D, S), F32, kind="ExternalOutput").ap())
    gated_block_kernel(nc, *args)
    r = run_bass_kernel_spmd(nc, [{"in_" + n: a for n, a in arrays.items()}], core_ids=[0])
    return r.results[0]["out_y"]
```
